# Optimizing a Trainium2 kernel written in Bass

```python
import numpy as np
import jax
import jax.numpy as jnp

def _softmax(x, axis=-1):
    return jax.nn.softmax(x, axis=axis)

def _gelu(x):
    return jax.nn.gelu(x, approximate=True)

def _silu(x):
    return jax.nn.silu(x)

def _sigmoid(x):
    return jax.nn.sigmoid(x)

def _layernorm(x, axis=-1, eps=1e-05):
    m = jnp.mean(x, axis=axis, keepdims=True)
    v = jnp.var(x, axis=axis, keepdims=True)
    return (x - m) / jnp.sqrt(v + eps)

def _scatter_add(tgt, idx, src, axis=0):
    return tgt.at[idx].add(src)

def _segment_sum(src, seg, n):
    return jax.ops.segment_sum(src, seg, n)
kernel_name = 'mk_sandwich_d1_jaxref_r8_326368'

def setup_inputs(seed: int=0):
    np.random.seed(seed)
    _w = jnp.asarray

    def _L0_attn_setup():
        import jax, jax.numpy as jnp
        import numpy as np
        NUM_HEADS = 16
        key = jax.random.key(seed)
        k1, k2, k3 = jax.random.split(key, 3)
        B, S, H = (2, 256, 256)
        x = jax.random.normal(k1, (B, S, H), dtype=jnp.float32)
        lim_qkv = (6.0 / (H + 3 * H)) ** 0.5
        lim_out = (6.0 / (H + H)) ** 0.5
        Wqkv = jax.random.uniform(k2, (3 * H, H), jnp.float32, -lim_qkv, lim_qkv)
        bqkv = jnp.zeros((3 * H,), jnp.float32)
        Wout = jax.random.uniform(k3, (H, H), jnp.float32, -lim_out, lim_out)
        bout = jnp.zeros((H,), jnp.float32)
        return {'x': x, 'Wqkv': Wqkv, 'bqkv': bqkv, 'Wout': Wout, 'bout': bout}
    _L0_attn_in = _L0_attn_setup()

    def _L0_ffn_setup():
        import jax, jax.numpy as jnp
        import numpy as np
        B, S, D, F, E, K = (2, 256, 256, 512, 8, 1)

        def _silu_mul(gu):
            g, u = jnp.split(gu, 2, axis=-1)
            return jax.nn.silu(g) * u

        def _moe_forward(hidden_states, router_w, w_gate_up, w_down, shared_gate_up, shared_down, top_k=K):
            b, s, d = hidden_states.shape
            x = hidden_states.reshape(-1, d)
            router_logits = x @ router_w.T
            topk_vals, topk_ids = jax.lax.top_k(router_logits, top_k)
            gate = jax.nn.sigmoid(topk_vals.astype(jnp.float32)).astype(x.dtype)
            xs = (x[:, None, :] * gate[:, :, None]).reshape(-1, d)
            ids_flat = topk_ids.reshape(-1)
            n_experts = w_gate_up.shape[0]

            def body(acc, inp):
                wg, wd, e = inp
                h = _silu_mul(xs @ wg)
                o = h @ wd
                mask = (ids_flat == e)[:, None]
                return (acc + jnp.where(mask, o, jnp.zeros((), o.dtype)), None)
            acc0 = jnp.zeros_like(xs)
            routed, _ = jax.lax.scan(body, acc0, (w_gate_up, w_down, jnp.arange(n_experts)))
            routed = routed.reshape(-1, top_k, d).sum(1)
            shared = _silu_mul(x @ shared_gate_up) @ shared_down
            return (routed + shared).reshape(b, s, d)
        key = jax.random.key(seed)
        ks = jax.random.split(key, 6)
        scale = 0.02
        return {'hidden_states': jax.random.normal(ks[0], (B, S, D), jnp.float32), 'router_w': jax.random.normal(ks[1], (E, D), jnp.float32) * scale, 'w_gate_up': jax.random.normal(ks[2], (E, D, 2 * F), jnp.float32) * scale, 'w_down': jax.random.normal(ks[3], (E, F, D), jnp.float32) * scale, 'shared_gate_up': jax.random.normal(ks[4], (D, 2 * F), jnp.float32) * scale, 'shared_down': jax.random.normal(ks[5], (F, D), jnp.float32) * scale}
    _L0_ffn_in = _L0_ffn_setup()
    _d = {'L0_attn_x': _L0_attn_in['x'], 'L0_attn_Wqkv': _L0_attn_in['Wqkv'], 'L0_attn_bqkv': _L0_attn_in['bqkv'], 'L0_attn_Wout': _L0_attn_in['Wout'], 'L0_attn_bout': _L0_attn_in['bout'], 'L0_ffn_router_w': _L0_ffn_in['router_w'], 'L0_ffn_w_gate_up': _L0_ffn_in['w_gate_up'], 'L0_ffn_w_down': _L0_ffn_in['w_down'], 'L0_ffn_shared_gate_up': _L0_ffn_in['shared_gate_up'], 'L0_ffn_shared_down': _L0_ffn_in['shared_down']}
    _x0 = _d['L0_attn_x']
    _d['L0_attn_x'] = jax.random.normal(jax.random.fold_in(jax.random.key(seed), 1), (2, 512, 256), dtype=_x0.dtype)
    del _x0
    return _d

def reference(L0_attn_x, L0_attn_Wqkv, L0_attn_bqkv, L0_attn_Wout, L0_attn_bout, L0_ffn_router_w, L0_ffn_w_gate_up, L0_ffn_w_down, L0_ffn_shared_gate_up, L0_ffn_shared_down):

    def _L0_attn_ref(x, Wqkv, bqkv, Wout, bout):
        import jax, jax.numpy as jnp
        import numpy as np
        NUM_HEADS = 16
        B, S, H = x.shape
        nh = NUM_HEADS
        hd = H // nh
        qkv = jnp.einsum('bsh,oh->bso', x, Wqkv) + bqkv
        q, k, v = jnp.split(qkv, 3, axis=-1)
        q = q.reshape(B, S, nh, hd).transpose(0, 2, 1, 3)
        k = k.reshape(B, S, nh, hd).transpose(0, 2, 1, 3)
        v = v.reshape(B, S, nh, hd).transpose(0, 2, 1, 3)
        scale = hd ** (-0.5)
        scores = jnp.einsum('bhqd,bhkd->bhqk', q, k) * scale
        causal = jnp.triu(jnp.ones((S, S), dtype=bool), k=1)
        scores = jnp.where(causal, -jnp.inf, scores)
        attn = jax.nn.softmax(scores, axis=-1)
        out = jnp.einsum('bhqk,bhkd->bhqd', attn, v)
        out = out.transpose(0, 2, 1, 3).reshape(B, S, H)
        return jnp.einsum('bsh,oh->bso', out, Wout) + bout

    def _L0_ffn_ref(hidden_states, router_w, w_gate_up, w_down, shared_gate_up, shared_down):
        import jax, jax.numpy as jnp
        import numpy as np
        B, S, D, F, E, K = (2, 256, 256, 512, 8, 1)

        def _silu_mul(gu):
            g, u = jnp.split(gu, 2, axis=-1)
            return jax.nn.silu(g) * u

        def _moe_forward(hidden_states, router_w, w_gate_up, w_down, shared_gate_up, shared_down, top_k=K):
            b, s, d = hidden_states.shape
            x = hidden_states.reshape(-1, d)
            router_logits = x @ router_w.T
            topk_vals, topk_ids = jax.lax.top_k(router_logits, top_k)
            gate = jax.nn.sigmoid(topk_vals.astype(jnp.float32)).astype(x.dtype)
            xs = (x[:, None, :] * gate[:, :, None]).reshape(-1, d)
            ids_flat = topk_ids.reshape(-1)
            n_experts = w_gate_up.shape[0]

            def body(acc, inp):
                wg, wd, e = inp
                h = _silu_mul(xs @ wg)
                o = h @ wd
                mask = (ids_flat == e)[:, None]
                return (acc + jnp.where(mask, o, jnp.zeros((), o.dtype)), None)
            acc0 = jnp.zeros_like(xs)
            routed, _ = jax.lax.scan(body, acc0, (w_gate_up, w_down, jnp.arange(n_experts)))
            routed = routed.reshape(-1, top_k, d).sum(1)
            shared = _silu_mul(x @ shared_gate_up) @ shared_down
            return (routed + shared).reshape(b, s, d)
        return _moe_forward(hidden_states, router_w, w_gate_up, w_down, shared_gate_up, shared_down)
    x = L0_attn_x
    x = x + _layernorm(_L0_attn_ref(_layernorm(x, axis=-1), L0_attn_Wqkv, L0_attn_bqkv, L0_attn_Wout, L0_attn_bout), axis=-1)
    x = x + _layernorm(_L0_ffn_ref(_layernorm(x, axis=-1), L0_ffn_router_w, L0_ffn_w_gate_up, L0_ffn_w_down, L0_ffn_shared_gate_up, L0_ffn_shared_down), axis=-1)
    return x

_drawn_inputs = setup_inputs


def setup_inputs(seed=0):
    import zlib

    import numpy as np

    out = dict(_drawn_inputs(seed))
    spreads = {'L0_attn_bqkv': (0.0, 0.1), 'L0_attn_bout': (0.0, 0.1)}
    factors = {}
    for name, (base, spread) in spreads.items():
        noise = np.random.default_rng([zlib.crc32(name.encode()), seed]).standard_normal(out[name].shape)
        drawn = base * np.exp(spread * noise) if base else spread * noise
        out[name] = jnp.asarray(drawn.astype(out[name].dtype))
    for name, factor in factors.items():
        out[name] = (out[name] * factor).astype(out[name].dtype)
    return out
```

```python
from contextlib import ExitStack

import concourse.bass as bass
from concourse import mybir

ALU = mybir.AluOpType
ACT = mybir.ActivationFunctionType
AX = mybir.AxisListType
F32 = mybir.dt.float32
F32R = mybir.dt.float32r
BF16 = mybir.dt.bfloat16
U32 = mybir.dt.uint32
ENGINE = mybir.EngineType

P = 128
NEG = -1e30
EPS = 1e-5


class Banks:

    def __init__(self, units, n_first=0, first=()):
        self.names = [n for n, _ in units]
        self.index = {n: i for i, n in enumerate(self.names)}
        self.who = dict(units)
        self.banks = [first[i % len(first)] if i < n_first else (i - n_first) % 8 for i in range(len(units))]

    def bank(self, name):
        return self.banks[self.index[name]]

    def filled(self, name):
        return self.index[name] + 1

    def emptied(self, name, engine):
        return sum(engine in self.who[n] for n in self.names[: self.index[name] + 1])

    def before(self, name):
        i = self.index[name]
        same = [j for j in range(i) if self.banks[j] == self.banks[i]]
        return self.names[same[-1]] if same else None


def build_block(nc, x, Wqkv, bqkv, Wout, bout, router_w, w_gate_up, w_down, shared_gate_up, shared_down, out):
    NB, S, D = x.shape
    H, HD = 16, 16
    NT = NB * S // P
    TB = S // P
    KC = D // P
    E, _, F2 = w_gate_up.shape
    F = F2 // 2
    FC = F // P
    SLOTS = NT + E - 1
    NG = 4
    SCALE = float(HD) ** -0.5
    assert (D, HD, S, TB, KC, E, F) == (256, 16, 512, 4, 2, 8, 512)

    ctx = ExitStack()
    with ctx:
        def sem(name):
            return ctx.enter_context(nc.semaphore(name))

        BASE = 16544
        KB = 1024

        def at(name, shape, dt, offset):
            return nc.alloc_sbuf_tensor_at(name, shape, dt, offset=BASE + offset)

        ROW = 2 * D + 1
        row_sb = at("row_sb", [P, NT, ROW], F32, -32)
        x_sb = row_sb[:, :, 0:D]
        tok_sb = row_sb[:, :, D:2 * D]
        left_sb = row_sb[:, :, 2 * D]
        tT_hi = at("tT_hi", [P, KC, NT * P], F32R, 16 * KB)
        tT_lo = at("tT_lo", [P, KC, NT * P], F32R, 24 * KB)
        rowT_hi = [at(f"rowT_hi{b}", [P, KC, S], F32R, (188, 16)[b] * KB) for b in range(NB)]
        rowT_lo = [at(f"rowT_lo{b}", [P, KC, S], F32R, (192, 24)[b] * KB) for b in range(NB)]
        q_op = [at(f"q_op{b}", [P, 8, S], F32R, (32 + 32 * b) * KB) for b in range(NB)]
        k_op = [[at(f"k_even{b}", [P, 8, S], F32R, (48 + 32 * b) * KB),
                 at(f"k_odd{b}", [P, 8, S], F32R, (188, 16)[b] * KB)] for b in range(NB)]
        sgu_raw = at("sgu_raw", [P, KC, F2], F32, 32 * KB)
        sgu_lo = at("sgu_lo", [P, KC, F2], F32R, 32 * KB)
        sdn_raw = at("sdn_raw", [P, FC, D], F32, 40 * KB)
        sdn_lo = at("sdn_lo", [P, FC, D], F32R, 40 * KB)
        sgu_hi = at("sgu_hi", [P, KC, F2], F32R, 44 * KB)
        sdn_hi = at("sdn_hi", [P, FC, D], F32R, 52 * KB)
        ysl = at("ysl", [P, 4, D], F32, 0)
        xin = at("xin", [P, 5, ROW], F32, 4 * KB)
        xinT_hi = at("xinT_hi", [P, 2, KC, P], F32R, 48 * KB)
        xinT_lo = at("xinT_lo", [P, 2, KC, P], F32R, 50 * KB)
        wsl_hi = [at(f"wsl_hi{i}", [P, KC, F2], F32R, (16, 24)[i] * KB) for i in range(2)]
        wsl_lo = [at(f"wsl_lo{i}", [P, KC, F2], F32R, (32, 56)[i] * KB) for i in range(2)]
        ysh_in = at("ysh_in", [P, 2, D], F32, 52 * KB)
        bo_bc = at("bo_bc", [P, D], F32, 63 * KB)
        wdn_sb = at("wdn_sb", [P, E * FC * D], F32, 64 * KB)
        v_sb = at("v_sb", [P, NT, H, 32], F32, 96 * KB)
        pT = at("pT", [P, 5, 1024], F32, 112 * KB)
        oT_sb = at("oT_sb", [P, 2, S], F32, 132 * KB)
        ysh_sb = at("ysh_sb", [P, NT, D], F32, 96 * KB)
        hT_hi = at("hT_hi", [P, FC, S], F32R, 104 * KB)
        hT_lo = at("hT_lo", [P, FC, S], F32R, 112 * KB)
        silu_sb = at("silu_sb", [P, 2, S], F32, 120 * KB)
        h_sb = at("h_sb", [P, 2, S], F32, 124 * KB)
        rhT = at("rhT", [P, 2, FC, P], F32, 128 * KB)
        woT_hi = at("woT_hi", [P, KC, D], F32R, 136 * KB)
        woT_lo = at("woT_lo", [P, KC, D], F32R, 138 * KB)
        wgu_sb = at("wgu_sb", [P, E * KC * F2], F32, 140 * KB)
        wqkv_raw = at("wqkv_raw", [P, 6, D], F32, 140 * KB)
        wout_raw = at("wout_raw", [P, 2, D], F32, 146 * KB)
        wT_hi = at("wT_hi", [P, KC, 3 * D], F32R, 148 * KB)
        wT_lo = at("wT_lo", [P, KC, 3 * D], F32R, 154 * KB)
        qk_hi = at("qk_hi", [P, 4, S], F32R, 160 * KB)
        qk_lo = at("qk_lo", [P, 4, S], F32R, 168 * KB)
        sel = at("sel", [P, 4, 4, P], F32R, 176 * KB)
        zero_sb = at("zero_sb", [P, ROW], F32, 112 * KB)
        bv_bc = at("bv_bc", [P, D], F32, 185 * KB)
        rw_sb = at("rw_sb", [P, D], F32, 186 * KB)
        bqk_raw = at("bqk_raw", [P, P], F32, 187 * KB)
        small = [204 * KB]

        def little(name, shape, dt, size):
            t = at(name, shape, dt, small[0])
            n = size
            for k in shape[1:]:
                n *= k
            small[0] += (n + 31) // 32 * 32
            return t

        ident = little("ident", [P, P], F32, 4)
        ident_b = little("ident_b", [P, P], BF16, 2)
        mask2 = little("mask2", [P, 2, P], BF16, 2)
        mT_hi = little("mT_hi", [16, P], F32R, 4)
        mT_lo = little("mT_lo", [16, P], F32R, 4)
        bqk = little("bqk", [P, 4], F32, 4)
        k_rows = little("k_rows", [P, 2], F32, 4)
        k_ones = little("k_ones", [P, 2], F32, 4)
        stats = little("stats", [P, NT, 6], F32, 4)
        mv = little("mv", [P, NT, 2], F32, 4)
        var_e = little("var_e", [P, NT], F32, 4)
        rstd = little("rstd", [P, NT], F32, 4)
        mhalf = little("mhalf", [P, NT], F32, 4)
        rwT_hi = little("rwT_hi", [P, KC, E], F32R, 4)
        rwT_lo = little("rwT_lo", [P, KC, E], F32R, 4)
        rmax = little("rmax", [P, 2, 16], F32, 4)
        orec = little("orec", [P, 16], F32, 4)
        assert BASE + small[0] <= 229344, small[0]
        small[0] = 132 * KB
        lt_b = little("lt_b", [P, P], BF16, 2)
        ones_b = little("ones_b", [P, P], BF16, 2)
        logits = little("logits", [P, NT, E], F32, 4)
        top = little("top", [P, NT], F32, 4)
        hit = little("hit", [P, NT, E], F32, 4)
        onehot = little("onehot", [P, NT, E], F32, 4)
        onehot_b = little("onehot_b", [P, NT, E], BF16, 2)
        first = little("first", [P, NT], F32, 4)
        gate = little("gate", [P, NT], F32, 4)
        desc = little("desc", [P, E], F32, 4)
        thr = little("thr", [P, E], F32, 4)
        slot_no = little("slot_no", [P, 16], F32, 4)
        over = little("over", [P, E, E], F32, 4)
        n_tiles = little("n_tiles", [P, E], F32, 4)
        ones_e = little("ones_e", [P, E], F32, 4)
        ends = little("ends", [P, E], F32, 4)
        base_t = little("base_t", [P, E], F32, 4)
        where = little("where", [P, NT, E], F32, 4)
        pos_f = little("pos_f", [P, NT], F32, 4)
        pos_u = little("pos_u", [P, NT], U32, 4)
        past = little("past", [P, 16, E], F32, 4)
        own_f = little("own_f", [P, 16], F32, 4)
        dest_u = little("dest_u", [P, 16], U32, 4)
        own_u = little("own_u", [P, 16], U32, 4)
        assert small[0] <= 136 * KB, small[0]

        ps = ctx.enter_context(nc.psum_tensor("ps", [P, 8, 512], F32))
        st_ps = [ps[:, 2 * i:2 * i + 2, :] for i in range(2)]
        o_ps = ps[:, 6, :]
        t_ps = ps[:, 7, :]

        xs_dram = nc.dram_tensor("xs_dram", (SLOTS * P, ROW), F32).ap()
        ysh_dram = nc.dram_tensor("ysh_dram", (SLOTS * P, D), F32).ap()

        x_loaded = [sem(f"x_loaded{b}") for b in range(NB)]
        w_loaded = sem("w_loaded")
        bias_loaded = sem("bias_loaded")
        bo_loaded = sem("bo_loaded")
        wgu_loaded = sem("wgu_loaded")
        wdn_loaded = sem("wdn_loaded")
        shared_loaded = sem("shared_loaded")
        slots_zeroed = sem("slots_zeroed")
        pool_step = sem("pool_step")
        dve_step = sem("dve_step")
        consts_ready = sem("consts_ready")
        rconsts_ready = sem("rconsts_ready")
        zero_ready = sem("zero_ready")
        var_ready = sem("var_ready")
        rstd_ready = sem("rstd_ready")
        norm_ready = sem("norm_ready")
        prep_filled = sem("prep_filled")
        prep_act = sem("prep_act")
        prep_dve = sem("prep_dve")
        m_filled = sem("m_filled")
        m_reduced = sem("m_reduced")
        mT_filled = sem("mT_filled")
        mT_act = sem("mT_act")
        mT_dve = sem("mT_dve")
        max_placed = sem("max_placed")
        st_filled = sem("st_filled")
        exp_done = sem("exp_done")
        causal_done = sem("causal_done")
        pv_done = sem("pv_done")
        oT_copied = sem("oT_copied")
        o_filled = sem("o_filled")
        o_normed = sem("o_normed")
        sh_hi = sem("sh_hi")
        sh_lo = sem("sh_lo")
        post_filled = sem("post_filled")
        post_act = sem("post_act")
        post_dve = sem("post_dve")
        hT_hi_ready = sem("hT_hi_ready")
        hT_lo_ready = sem("hT_lo_ready")
        onehot_ready = sem("onehot_ready")
        top_ready = sem("top_ready")
        gate_ready = sem("gate_ready")
        gated_ready = sem("gated_ready")
        pos_ready = sem("pos_ready")
        owner_ready = sem("owner_ready")
        scattered = sem("scattered")
        wsl_hi_ready = sem("wsl_hi_ready")
        wsl_lo_ready = sem("wsl_lo_ready")
        ysh_scattered = sem("ysh_scattered")
        xin_loaded = [sem(f"xin_loaded{i}") for i in range(5)]
        ysh_loaded = [sem(f"ysh_loaded{i}") for i in range(2)]
        last_norm_ready = sem("last_norm_ready")
        final_ready = sem("final_ready")
        out_scattered = [sem(f"out_scattered{i}") for i in range(4)]

        prep_units = [(f"W{i}", "AD") for i in range(3)] + [("WO", "AD"), ("RW", "AD")]
        for b in range(NB):
            prep_units += [(f"X{b}{kc}", "AD") for kc in range(KC)]
            prep_units += [(f"QK{b}{mt}", "AD") for mt in range(4)]
            prep_units += [(f"V{b}{i}", "D") for i in range(2)]
            for p in range(8):
                prep_units += [(f"SQ{b}{p}", "D" if p % 2 else "A"), (f"SK{b}{p}", "AD")]
        prep = Banks(prep_units)

        def attn_out_units(b):
            return [(f"A{b}{kc}", "AD") for kc in range(KC)] + [(f"OP{b}{i}", "D") for i in range(2)]

        def router_units(b):
            return [(f"X{b}{kc}", "AD") for kc in range(KC)] + [(f"R{b}", "D")]

        def hidden_units(b, fts):
            return [(f"{n}{b}{ft}", who) for ft in fts for n, who in (("G", "A"), ("U", "D"))]

        def down_units(b):
            return [(f"DN{b}{i}", "A") for i in range(2)]

        post_units = attn_out_units(0) + router_units(0)
        n_early = len(post_units)
        post_units += hidden_units(0, [0]) + attn_out_units(1)[:2] + hidden_units(0, [1]) + attn_out_units(1)[2:]
        post_units += hidden_units(0, [2, 3]) + down_units(0) + router_units(1)
        post_units += hidden_units(1, [0]) + [("RK", "D")] + hidden_units(1, [1, 2, 3]) + down_units(1)
        post_units += [("xt0", "AD"), ("g0", "A"), ("u0", "D"), ("xt1", "AD")]
        for s in range(SLOTS):
            if s + 1 < SLOTS:
                post_units += [(f"g{s + 1}", "A")]
            post_units += [(f"ht{s}", "A")]
            if s + 2 < SLOTS:
                post_units += [(f"xt{s + 2}", "AD")]
            if s + 1 < SLOTS:
                post_units += [(f"u{s + 1}", "D")]
            post_units += [(f"dn{s}", "D")]
        post = Banks(post_units, n_early, (4, 5))

        GROUPS = NB * NG
        LAG = 3
        M_BANKS = 11

        def m_plan():
            return [([0], 3), ([1], 3), ([2], 3), ([3], 3), ([0], 2), ([1], 2), ([2], 2), ([3], 2),
                    ([0, 2], 1), ([1, 3], 1), ([0, 2, 1, 3], 0)]

        def st_plan(u):
            if u < 2:
                return [(2 * u + i, 0, i, 0) for i in range(2)]
            if u < 4:
                return [(2 * (u - 2) + i, kt, i, c) for i in range(2) for kt, c in ((3, 0), (1, P))]
            return [(2 * i + k, 2, i, 256 * k) for i in range(2) for k in range(2)]

        def pt_place(j, kt):
            for u in range(5):
                for j2, kt2, i, c in st_plan(u):
                    if (j2, kt2) == (j, kt):
                        return u, 512 * i + c

        def m_bank(n):
            return (4, 5, 0, 1, 2, 3)[n % 6] if n < M_BANKS * LAG else 4 + n % 2

        def m_before(n):
            same = [k for k in range(max(n - 6, 0), n) if m_bank(k) == m_bank(n)]
            return same[-1] if same else None

        def owner(s, engine):
            return nc.values_load(own_u[0:1, s:s + 1], engines=(engine,), min_val=0, max_val=E - 1,
                                  skip_runtime_bounds_check_because="own_u is clamped to 0..E-1 when it is written")

        def owned_half(e, half):
            return wgu_sb[:, bass.ds(e * (KC * F2), KC * F2)].rearrange("p (k n) -> p k n", k=KC)[:, :, F * half:F * half + F]

        MT_ORDER = [2 * (j % 2) + j // 2 for j in range(4)]

        block = ctx.enter_context(nc.Block())

        def row_broadcast(ap, lo, n):
            return bass.AP(tensor=ap.tensor, offset=lo, ap=[[0, P], [1, n]])

        @block.sync
        def _(sp):
            for b in range(NB):
                sp.dma_start(x_sb[:, TB * b:TB * b + TB, :], x[b].rearrange("(t p) d -> p t d", p=P)) \
                    .then_inc(x_loaded[b], 16)
            sp.wait_ge(x_loaded[1], 16)
            sp.wait_ge(w_loaded, 64)
            sp.wait_ge(zero_ready, 1)
            for rows, width in ((xs_dram, ROW), (ysh_dram, D)):
                sp.dma_start(rows.rearrange("(s p) d -> p s d", p=P),
                             zero_sb[:, 0:width].unsqueeze(1).to_broadcast([P, SLOTS, width])).then_inc(slots_zeroed, 16)
            sp.wait_ge(prep_filled, len(prep_units))
            sp.wait_ge(prep_dve, prep.emptied("SK17", "D"))
            sp.wait_ge(prep_act, prep.emptied("SK17", "A"))
            wgu_v = wgu_sb[:, :].rearrange("p (e k n) -> p e k n", e=E, k=KC)

            def load_wgu(experts):
                for e in experts:
                    sp.dma_start(wgu_v[:, e, :, :], w_gate_up[e].rearrange("(k p) n -> p k n", p=P)).then_inc(wgu_loaded, 16)

            for g in range(GROUPS):
                b, gi = divmod(g, NG)
                sp.wait_ge(mT_act, g + 1)
                sp.wait_ge(mT_dve, g + 1)
                for par in range(2):
                    for row, src in ((48, mT_hi), (49, mT_lo)):
                        r = 64 * par + row
                        dst = q_op[b][r:r + 1, 2 * gi:2 * gi + 2, :].bitcast(F32)
                        sp.dma_start(dst.rearrange("o j (t k) -> o (j t) k", k=P),
                                     src[8 * par:8 * par + 8, :].bitcast(F32)).then_inc(max_placed, 16)
                if g < 3:
                    load_wgu((2 * g, 2 * g + 1))
                if g == 5:
                    sp.wait_ge(st_filled, 5 * NG)
                    sp.dma_start(sgu_raw[:, :, :], shared_gate_up.rearrange("(k p) n -> p k n", p=P)).then_inc(shared_loaded, 16)
                    sp.dma_start(sdn_raw[:, :, :], shared_down.rearrange("(k p) n -> p k n", p=P)).then_inc(shared_loaded, 16)
                    load_wgu((E - 1,))
                    sp.dma_start(bo_bc[:, :], row_broadcast(bout, 0, D)).then_inc(bo_loaded, 16)
            sp.wait_ge(st_filled, 5 * GROUPS)
            wdn_v = wdn_sb[:, :].rearrange("p (e k n) -> p e k n", e=E, k=FC)
            for e in range(E):
                sp.dma_start(wdn_v[:, e, :, :], w_down[e].rearrange("(k p) n -> p k n", p=P)).then_inc(wdn_loaded, 16)
            sp.wait_ge(post_filled, post.filled("U03"))
            load_wgu((E - 2,))
            sp.wait_ge(scattered, 16 * NT)

            def load_rows(s):
                if s >= 5:
                    sp.wait_ge(final_ready, s - 4)
                sp.dma_start(xin[:, s % 5, :], xs_dram[s * P:s * P + P, :]).then_inc(xin_loaded[s % 5], 16)

            def load_shared(s):
                if s >= 2:
                    sp.wait_ge(post_dve, post.emptied(f"dn{s - 2}", "D"))
                sp.dma_start(ysh_in[:, s % 2, :], ysh_dram[s * P:s * P + P, :]).then_inc(ysh_loaded[s % 2], 16)

            for s in range(5):
                load_rows(s)
            sp.wait_ge(ysh_scattered, 16 * NT)
            for s in range(2):
                load_shared(s)
            for s in range(SLOTS):
                if s + 2 < SLOTS:
                    load_shared(s + 2)
                if s + 5 < SLOTS:
                    load_rows(s + 5)

        @block.gpsimd
        def _(pool):
            steps = 0

            def step(ins):
                nonlocal steps
                steps += 1
                ins.then_inc(pool_step, 1)

            step(pool.memset(ident[:, :], 0.0))
            step(pool.memset(mhalf[:, :], -0.5))
            pool.memset(zero_sb[:, :], 0.0).then_inc(zero_ready, 1)
            pool.wait_ge(pool_step, steps)
            step(pool.affine_select(out=ident[:, :], in_=ident[:, :], compare_op=ALU.not_equal, fill=1.0,
                                    base=0, pattern=[[-1, P]], channel_multiplier=1))
            pool.wait_ge(pool_step, steps)
            pool.memset(k_ones[:, :], 0.0).then_inc(consts_ready, 1)

            norms = 0

            def rstd_of(tiles):
                nonlocal norms
                norms += 1
                pool.wait_ge(var_ready, norms)
                pool.tensor_tensor(rstd[:, tiles], var_e[:, tiles], mhalf[:, tiles], ALU.pow).then_inc(rstd_ready, 1)

            rstd_of(slice(0, TB))
            pool.iota(left_sb, [[-P, NT]], base=NT * P, channel_multiplier=-1,
                      allow_small_or_imprecise_dtypes=True).then_inc(consts_ready, 1)
            step(pool.memset(sel[:, :, :, :].bitcast(F32), 0.0))
            step(pool.memset(mask2[:, :, :], 0.0))
            step(pool.memset(ident_b[:, :], 0.0))
            step(pool.memset(k_rows[:, :], 1.0))
            step(pool.memset(v_sb[:, :, :, 16:32], 1.0))
            pool.wait_ge(pool_step, steps)
            sel_v = sel[:, :, :, :].rearrange("p m h (r x) -> p m (h r) x", r=2)
            for m, part in ((0, 0), (0, 2), (1, 1), (2, 0), (2, 1), (3, 2)):
                view = sel_v[:, m, :, 16 * part:16 * part + 16]
                step(pool.affine_select(out=view, in_=view.bitcast(F32), compare_op=ALU.not_equal, fill=1.0,
                                        base=0, pattern=[[-16, 8], [-1, 16]], channel_multiplier=1))
            step(pool.affine_select(out=ident_b[:, :], in_=ident_b[:, :], compare_op=ALU.not_equal, fill=1.0,
                                    base=0, pattern=[[-1, P]], channel_multiplier=1))
            step(pool.affine_select(out=mask2[:, :, :], in_=mask2[:, :, :], compare_op=ALU.is_ge, fill=NEG,
                                    base=0, pattern=[[0, 2], [-1, P]], channel_multiplier=1))
            step(pool.affine_select(out=k_rows[:, 0:1], in_=k_rows[:, 0:1], compare_op=ALU.is_ge, fill=0.0,
                                    base=63, pattern=[[0, 1]], channel_multiplier=-1))
            step(pool.affine_select(out=k_rows[:, 1:2], in_=k_rows[:, 1:2], compare_op=ALU.is_ge, fill=0.0,
                                    base=-64, pattern=[[0, 1]], channel_multiplier=1))
            for r in (48, 49):
                pool.wait_ge(pool_step, steps)
                step(pool.affine_select(out=k_ones[:, :], in_=k_ones[:, :], compare_op=ALU.not_equal, fill=1.0,
                                        base=-r, pattern=[[-64, 2]], channel_multiplier=1))
            pool.wait_ge(pool_step, steps)
            pool.memset(rmax[:, :, :], 0.0).then_inc(consts_ready, 1)
            rstd_of(slice(TB, 2 * TB))

            def causal(g, u):
                pool.wait_ge(exp_done, 5 * g + u + 1)
                if u < 2:
                    view = pT[:, u, :].rearrange("p (i c) -> p i c", i=2)[:, :, 0:P]
                    pattern = [[0, 2], [1, P]]
                elif u < 4:
                    view = pT[:, u, :].rearrange("p (i c) -> p i c", i=2)[:, :, 0:2 * P]
                    pattern = [[0, 2], [0, 2], [1, P]]
                else:
                    view = pT[:, u, :].rearrange("p (i c) -> p i c", i=4)[:, :, 0:P]
                    pattern = [[0, 4], [1, P]]
                pool.affine_select(out=view, in_=view, compare_op=ALU.is_ge, fill=0.0, base=0,
                                   pattern=pattern, channel_multiplier=-1).then_inc(causal_done, 1)

            for s in range(LAG, GROUPS + LAG):
                for u in range(5):
                    causal(s - LAG, u)
                    if (s, u) in ((GROUPS + 1, 1), (GROUPS + 2, 0)):
                        rstd_of(slice(0, TB))
            pool.wait_ge(o_filled, GROUPS)
            step(pool.memset(lt_b[:, :], 1.0))
            step(pool.memset(ones_b[:, :], 1.0))
            step(pool.memset(ones_e[:, :], 1.0))
            step(pool.iota(desc[:, :], [[-1, E]], base=E, channel_multiplier=0, allow_small_or_imprecise_dtypes=True))
            step(pool.iota(thr[:, :], [[P, E]], base=0, channel_multiplier=0, allow_small_or_imprecise_dtypes=True))
            step(pool.iota(slot_no[:, :], [[1, 16]], base=0, channel_multiplier=0, allow_small_or_imprecise_dtypes=True))
            pool.wait_ge(pool_step, steps)
            pool.affine_select(out=lt_b[:, :], in_=lt_b[:, :], compare_op=ALU.is_gt, fill=0.0, base=0,
                               pattern=[[1, P]], channel_multiplier=-1).then_inc(rconsts_ready, 1)
            rstd_of(slice(TB, 2 * TB))
            rstd_of(slice(TB, 2 * TB))
            pool.wait_ge(slots_zeroed, 32)
            pool.wait_ge(pos_ready, 1)
            for t in range(NT):
                pool.wait_ge(gated_ready, t + 1)
                pool.indirect_dma_start(xs_dram, bass.IndirectOffsetOnAxis(pos_u[:, t:t + 1], 0),
                                        row_sb[:, t, :], None).then_inc(scattered, 16)
            for t in range(NT):
                pool.wait_ge(post_act, post.emptied(f"DN{t // TB}{t % TB // 2}", "A"))
                pool.indirect_dma_start(ysh_dram, bass.IndirectOffsetOnAxis(pos_u[:, t:t + 1], 0),
                                        ysh_sb[:, t, :], None).then_inc(ysh_scattered, 16)
            out_rows = out.rearrange("b s d -> (b s) d")
            for s in range(SLOTS):
                i, y, rows = s % NT, ysl[:, s % 4, :], xin[:, s % 5, :]
                pool.wait_ge(xin_loaded[s % 5], 16 * (s // 5 + 1))
                step(pool.tensor_scalar(dest_u[:, s:s + 1], rows[:, 2 * D:ROW], -1.0, float(NT * P), ALU.mult, ALU.add))
                rstd_of(slice(i, i + 1))
                pool.wait_ge(last_norm_ready, s + 1)
                pool.tensor_tensor(y, y, rows[:, 0:D], ALU.add).then_inc(final_ready, 1)
                pool.wait_ge(final_ready, s + 1)
                pool.indirect_dma_start(out_rows, bass.IndirectOffsetOnAxis(dest_u[:, s:s + 1], 0), ysl[:, s % 4, :], None,
                                        bounds_check=NT * P - 1, oob_is_err=False).then_inc(out_scattered[s % 4], 16)
            for i in range(4):
                pool.wait_ge(out_scattered[i], 16 * ((SLOTS - i + 3) // 4))

        @block.scalar
        def _(act):
            act.dma_start(wqkv_raw[:, :, :], Wqkv.rearrange("(r p) d -> p r d", p=P)).then_inc(w_loaded, 16)
            act.dma_start(wout_raw[:, :, :], Wout.rearrange("(r p) d -> p r d", p=P)).then_inc(w_loaded, 16)
            act.dma_start(rw_sb[0:E, :], router_w).then_inc(w_loaded, 16)
            act.dma_start(bqk_raw[0:4, :], bqkv[0:2 * D].rearrange("(m p) -> m p", p=P)).then_inc(w_loaded, 16)
            act.dma_start(bv_bc[:, :], row_broadcast(bqkv, 2 * D, D)).then_inc(bias_loaded, 16)

            def prep_unit(name, out_ap, in_ap, **kw):
                act.wait_ge(prep_filled, prep.filled(name))
                act.activation(out_ap, in_ap, ACT.Identity if kw else ACT.Copy, **kw).then_inc(prep_act, 1)

            wT_f = wT_hi[:, :, :].rearrange("p k n -> p (k n)")
            for i in range(3):
                prep_unit(f"W{i}", wT_f[:, 512 * i:512 * i + 512], ps[:, prep.bank(f"W{i}"), :])
            prep_unit("WO", woT_hi[:, :, :].rearrange("p k n -> p (k n)"), ps[:, prep.bank("WO"), :])
            act.wait_ge(prep_filled, prep.filled("RW"))
            act.activation(bqk[:, :], ps[:, prep.bank("RW"), KC * E:KC * E + 4], ACT.Copy).then_inc(bias_loaded, 1)
            prep_unit("RW", rwT_hi[:, :, :].rearrange("p k n -> p (k n)"), ps[:, prep.bank("RW"), 0:KC * E])
            act.wait_ge(bias_loaded, 17)
            for b in range(NB):
                for kc in range(KC):
                    prep_unit(f"X{b}{kc}", tT_hi[:, kc, S * b:S * b + S], ps[:, prep.bank(f"X{b}{kc}"), :])
                for mt in range(4):
                    prep_unit(f"QK{b}{mt}", qk_hi[:, mt, :], ps[:, prep.bank(f"QK{b}{mt}"), :], bias=bqk[:, mt:mt + 1])
                act.wait_ge(consts_ready, 3)
                for p in range(8):
                    if p % 2 == 0:
                        prep_unit(f"SQ{b}{p}", q_op[b][:, p, :], ps[:, prep.bank(f"SQ{b}{p}"), :])
                    prep_unit(f"SK{b}{p}", k_op[b][0][:, p, :], ps[:, prep.bank(f"SK{b}{p}"), :],
                              bias=k_ones[:, 0:1], scale=k_rows[:, 0:1])

            def exps(g, u):
                n = 5 * g + u
                act.wait_ge(st_filled, n + 1)
                if n == 0:
                    act.wait_ge(slots_zeroed, 32)
                if g >= 1:
                    act.wait_ge(pv_done, 4 * (g - 1) + (1, 1, 3, 3, 4)[u])
                act.activation(pT[:, u, :], st_ps[n % 2].rearrange("p i c -> p (i c)"), ACT.Exp, scale=SCALE) \
                    .then_inc(exp_done, 1)

            def oT_copy(g):
                act.wait_ge(pv_done, 4 * g + 4)
                if g >= 2:
                    act.wait_ge(o_filled, g - 1)
                act.activation(oT_sb[:, g % 2, :], o_ps, ACT.Copy).then_inc(oT_copied, 1)

            def max_hi(g):
                act.wait_ge(mT_filled, g + 1)
                if g >= 1:
                    act.wait_ge(max_placed, 64 * g)
                act.activation(mT_hi[:, :], t_ps[0:16, 0:P], ACT.Copy, scale=-1.0).then_inc(mT_act, 1)

            def shared_hi(cs):
                for c in cs:
                    act.wait_ge(shared_loaded, 32)
                    if c < 4:
                        k, half = divmod(c, 2)
                        o, r = (w[:, k, 512 * half:512 * half + 512] for w in (sgu_hi, sgu_raw))
                    else:
                        o, r = (w[:, 2 * (c - 4):2 * (c - 4) + 2, :] for w in (sdn_hi, sdn_raw))
                    act.activation(o, r, ACT.Copy).then_inc(sh_hi, 1)

            def post_unit(name, out_ap, in_ap, func=ACT.Copy):
                act.wait_ge(post_filled, post.filled(name))
                return act.activation(out_ap, in_ap, func).then_inc(post_act, 1)

            def transposed_hi(b, name):
                for kc in range(KC):
                    post_unit(f"{name}{b}{kc}", rowT_hi[b][:, kc, :], ps[:, post.bank(f"{name}{b}{kc}"), :])

            for s in range(GROUPS + LAG + 1):
                e = s - LAG
                if 0 <= e < GROUPS:
                    exps(e, 0)
                if 0 <= e - 1 < GROUPS:
                    oT_copy(e - 1)
                if 0 <= s - 1 < GROUPS:
                    max_hi(s - 1)
                if 0 <= e < GROUPS:
                    exps(e, 1)
                    if s == GROUPS:
                        transposed_hi(0, "A")
                    for u in range(2, 5):
                        exps(e, u)
                if s == GROUPS + 2:
                    transposed_hi(0, "X")
                if GROUPS <= s < GROUPS + 3:
                    shared_hi([2 * (s - GROUPS), 2 * (s - GROUPS) + 1])


            def shared_hidden(b, ft):
                post_unit(f"G{b}{ft}", silu_sb[:, ft % 2, :], ps[:, post.bank(f"G{b}{ft}"), :], ACT.Silu)

            def shared_hidden_hi(b, ft):
                act.wait_ge(post_dve, post.emptied(f"U{b}{ft}", "D"))
                if b == 1:
                    act.wait_ge(post_filled, post.filled("DN01"))
                act.activation(hT_hi[:, ft, :], h_sb[:, ft % 2, :], ACT.Copy).then_inc(hT_hi_ready, 1)

            def shared_units(b, fts):
                for ft in fts:
                    if b or ft >= 2:
                        bb, ff = (b, ft - 2) if ft >= 2 else (b - 1, ft + 2)
                        act.wait_ge(post_dve, post.emptied(f"U{bb}{ff}", "D"))
                    shared_hidden(b, ft)
                    if ft >= 1:
                        shared_hidden_hi(b, ft - 1)
                    if ft == FC - 1:
                        shared_hidden_hi(b, ft)

            def shared_down(b):
                for i in range(2):
                    name = f"DN{b}{i}"
                    post_unit(name, ysh_sb[:, TB * b + 2 * i:TB * b + 2 * i + 2, :].rearrange("p t d -> p (t d)"),
                              ps[:, post.bank(name), :])

            shared_units(0, [0])
            transposed_hi(1, "A")
            shared_units(0, [1, 2, 3])
            shared_down(0)
            transposed_hi(1, "X")
            act.wait_ge(top_ready, 1)
            act.activation(gate[:, :], top[:, :], ACT.Sigmoid).then_inc(gate_ready, 1)
            shared_units(1, [0, 1, 2, 3])

            def slot_xT(s):
                if s >= 2:
                    act.wait_ge(post_filled, post.filled(f"u{s - 2}"))
                post_unit(f"xt{s}", xinT_hi[:, s % 2, :, :].rearrange("p k t -> p (k t)"),
                          ps[:, post.bank(f"xt{s}"), 0:KC * P])

            def slot_silu(s):
                if s >= 2:
                    act.wait_ge(post_dve, post.emptied(f"u{s - 2}", "D"))
                else:
                    act.wait_ge(post_dve, post.emptied(f"U1{FC - 2 + s}", "D"))
                post_unit(f"g{s}", silu_sb[:, s % 2, :], ps[:, post.bank(f"g{s}"), :], ACT.Silu)

            def slot_weights(s, e, half):
                act.wait_ge(post_filled, post.filled(f"{'gu'[half]}{s - 2}" if s >= 2 else f"U1{FC - 1}"))
                act.activation(wsl_hi[s % 2][:, :, F * half:F * half + F], owned_half(e, half), ACT.Copy) \
                    .then_inc(wsl_hi_ready, 1)

            def slot_hT(s):
                if s >= 2:
                    act.wait_ge(post_filled, post.filled(f"dn{s - 2}"))
                post_unit(f"ht{s}", rhT[:, s % 2, :, :].rearrange("p k t -> p (k t)"), ps[:, post.bank(f"ht{s}"), :])

            act.wait_ge(owner_ready, 1)
            act.wait_ge(wgu_loaded, 16 * E)
            owners = [owner(s, ENGINE.Activation) for s in range(SLOTS)]
            for s in range(2):
                e = owners[s]
                slot_weights(s, e, 0)
                slot_weights(s, e, 1)
                if s == 0:
                    shared_down(1)
            slot_xT(0)
            slot_silu(0)
            slot_xT(1)
            for s in range(SLOTS):
                if s + 2 < SLOTS:
                    e = owners[s + 2]
                    slot_weights(s + 2, e, 0)
                if s + 1 < SLOTS:
                    slot_silu(s + 1)
                slot_hT(s)
                if s + 2 < SLOTS:
                    slot_xT(s + 2)
                    slot_weights(s + 2, e, 1)

        @block.vector
        def _(dve):
            steps = 0

            def step(ins):
                nonlocal steps
                steps += 1
                return ins.then_inc(dve_step, 1)

            def settle():
                dve.wait_ge(dve_step, steps)

            norms = 0

            def norm_stats(src, tiles):
                nonlocal norms
                for t in tiles:
                    step(dve.bn_stats(stats[:, t, :], src[:, t, :]))
                settle()
                for t in tiles:
                    step(dve.bn_aggr(mv[:, t, :], stats[:, t, :]))
                settle()
                lo, hi = tiles[0], tiles[-1] + 1
                dve.tensor_scalar(var_e[:, lo:hi], mv[:, lo:hi, 1], EPS, None, ALU.add).then_inc(var_ready, 1)
                norms += 1

            def norm_apply(dst, src, t):
                return dve.tensor_scalar(dst[:, t, :], src[:, t, :], mv[:, t, 0:1], rstd[:, t:t + 1],
                                         ALU.subtract, ALU.mult)

            def batch_tiles(b):
                return list(range(TB * b, TB * b + TB))

            def prep_lo(name, out_ap, hi_ap, n=512):
                dve.wait_ge(prep_act, prep.emptied(name, "A"))
                dve.tensor_tensor(out_ap, ps[:, prep.bank(name), 0:n], hi_ap, ALU.subtract).then_inc(prep_dve, 1)

            def first_norm(b):
                dve.wait_ge(x_loaded[b], 16)
                norm_stats(x_sb, batch_tiles(b))
                dve.wait_ge(rstd_ready, norms)
                for t in batch_tiles(b):
                    norm_apply(tok_sb, x_sb, t).then_inc(norm_ready, 1)

            first_norm(0)
            wT_fh = wT_hi[:, :, :].rearrange("p k n -> p (k n)").bitcast(F32)
            wT_fl = wT_lo[:, :, :].rearrange("p k n -> p (k n)")
            for i in range(3):
                prep_lo(f"W{i}", wT_fl[:, 512 * i:512 * i + 512], wT_fh[:, 512 * i:512 * i + 512])
            prep_lo("WO", woT_lo[:, :, :].rearrange("p k n -> p (k n)"),
                    woT_hi[:, :, :].rearrange("p k n -> p (k n)").bitcast(F32))
            prep_lo("RW", rwT_lo[:, :, :].rearrange("p k n -> p (k n)"),
                    rwT_hi[:, :, :].rearrange("p k n -> p (k n)").bitcast(F32), KC * E)
            dve.wait_ge(bias_loaded, 17)
            for b in range(NB):
                for kc in range(KC):
                    prep_lo(f"X{b}{kc}", tT_lo[:, kc, S * b:S * b + S], tT_hi[:, kc, S * b:S * b + S].bitcast(F32))
                if b == 0:
                    first_norm(1)
                for mt in range(4):
                    name = f"QK{b}{mt}"
                    dve.wait_ge(prep_act, prep.emptied(name, "A"))
                    dve.scalar_tensor_tensor(out=qk_lo[:, mt, :], in0=ps[:, prep.bank(name), :], scalar=bqk[:, mt:mt + 1],
                                             in1=qk_hi[:, mt, :].bitcast(F32), op0=ALU.add, op1=ALU.subtract) \
                        .then_inc(prep_dve, 1)
                for i in range(2):
                    name = f"V{b}{i}"
                    dve.wait_ge(prep_filled, prep.filled(name))
                    for n in range(2):
                        t = TB * b + 2 * i + n
                        ins = dve.tensor_tensor(v_sb[:, t, :, 0:HD],
                                                ps[:, prep.bank(name), D * n:D * n + D].rearrange("p (h d) -> p h d", d=HD),
                                                bv_bc[:, :].rearrange("p (h d) -> p h d", d=HD), ALU.add)
                    ins.then_inc(prep_dve, 1)
                dve.wait_ge(consts_ready, 3)
                for p in range(8):
                    name = f"SQ{b}{p}"
                    if p % 2:
                        dve.wait_ge(prep_filled, prep.filled(name))
                        dve.tensor_copy(q_op[b][:, p, :], ps[:, prep.bank(name), :]).then_inc(prep_dve, 1)
                    name = f"SK{b}{p}"
                    dve.wait_ge(prep_act, prep.emptied(name, "A"))
                    dve.tensor_scalar(k_op[b][1][:, p, :], ps[:, prep.bank(name), :], k_rows[:, 1:2], k_ones[:, 1:2],
                                      ALU.mult, ALU.add).then_inc(prep_dve, 1)

            dve.wait_ge(consts_ready, 3)

            def maxima(g, banks):
                for i in banks:
                    heads, qt = m_plan()[i]
                    n = M_BANKS * g + i
                    w = P * (qt + 1)
                    dve.wait_ge(m_filled, n + 1)
                    if g >= 2:
                        dve.wait_ge(mT_filled, g - 1)
                    c = 4 * MT_ORDER[heads[0]] + qt
                    dve.tensor_reduce(rmax[:, g % 2, c:c + 4 * (len(heads) - 1) + 1:4],
                                      ps[:, m_bank(n), :][:, 0:w * len(heads)].rearrange("p (h c) -> p h c", c=w),
                                      AX.X, ALU.max).then_inc(m_reduced, 1)

            def max_lo(g):
                dve.wait_ge(mT_act, g + 1)
                dve.scalar_tensor_tensor(out=mT_lo[:, :], in0=t_ps[0:16, 0:P], scalar=-1.0,
                                         in1=mT_hi[:, :].bitcast(F32), op0=ALU.mult, op1=ALU.subtract) \
                    .then_inc(mT_dve, 1)

            def normalise(g):
                b, gi = divmod(g, NG)
                dve.wait_ge(o_filled, g + 1)
                blocks = t_ps.rearrange("p (q j c) -> p q j c", q=TB, j=4)
                settle()
                step(dve.reciprocal(orec[:, :].rearrange("p (q j) -> p q j", j=4), blocks[:, :, :, HD]))
                settle()
                dst = tok_sb[:, TB * b:TB * b + TB, 64 * gi:64 * gi + 64].rearrange("p q (j d) -> p q j d", d=HD)
                dve.tensor_tensor(dst, blocks[:, :, :, 0:HD],
                                  orec[:, :].rearrange("p (q j) -> p q j", j=4).unsqueeze(3).to_broadcast([P, TB, 4, HD]),
                                  ALU.mult).then_inc(o_normed, 1)

            def transposed_lo(b, name):
                for kc in range(KC):
                    unit = f"{name}{b}{kc}"
                    dve.wait_ge(post_act, post.emptied(unit, "A"))
                    dve.tensor_tensor(rowT_lo[b][:, kc, :], ps[:, post.bank(unit), :],
                                      rowT_hi[b][:, kc, :].bitcast(F32), ALU.subtract).then_inc(post_dve, 1)

            def projected(b):
                dve.wait_ge(bo_loaded, 16)
                for i in range(2):
                    name = f"OP{b}{i}"
                    t = TB * b + 2 * i
                    dve.wait_ge(post_filled, post.filled(name))
                    dve.tensor_tensor(tok_sb[:, t:t + 2, :], ps[:, post.bank(name), :].rearrange("p (t d) -> p t d", t=2),
                                      bo_bc[:, :].unsqueeze(1).to_broadcast([P, 2, D]), ALU.add).then_inc(post_dve, 1)
                dve.wait_ge(post_dve, post.emptied(f"OP{b}1", "D"))
                norm_stats(tok_sb, batch_tiles(b))

            def residual(b):
                dve.wait_ge(rstd_ready, norms)
                for t in batch_tiles(b):
                    step(norm_apply(tok_sb, tok_sb, t))
                settle()
                for t in batch_tiles(b):
                    step(dve.tensor_tensor(x_sb[:, t, :], x_sb[:, t, :], tok_sb[:, t, :], ALU.add))
                settle()
                norm_stats(x_sb, batch_tiles(b))

            def second_norm(b):
                dve.wait_ge(rstd_ready, norms)
                for t in batch_tiles(b):
                    norm_apply(tok_sb, x_sb, t).then_inc(norm_ready, 1)

            def take_logits(b):
                name = f"R{b}"
                dve.wait_ge(post_filled, post.filled(name))
                dve.tensor_copy(logits[:, TB * b:TB * b + TB, :].rearrange("p t e -> p (t e)"),
                                ps[:, post.bank(name), 0:TB * E]).then_inc(post_dve, 1)

            def shared_lo(n):
                for c in n:
                    dve.wait_ge(sh_hi, c + 1)
                    if c < 4:
                        k, half = divmod(c, 2)
                        o, r, h = (w[:, k, 512 * half:512 * half + 512] for w in (sgu_lo, sgu_raw, sgu_hi))
                    else:
                        o, r, h = (w[:, 2 * (c - 4):2 * (c - 4) + 2, :] for w in (sdn_lo, sdn_raw, sdn_hi))
                    dve.tensor_tensor(o, r, h.bitcast(F32), ALU.subtract).then_inc(sh_lo, 1)

            for s in range(GROUPS + LAG + 1):
                if s < GROUPS:
                    maxima(s, range(0, 3))
                if 0 <= s - 1 < GROUPS:
                    max_lo(s - 1)
                if s < GROUPS:
                    maxima(s, range(3, 9))
                if s == GROUPS:
                    transposed_lo(0, "A")
                if s == GROUPS + 1:
                    shared_lo([0, 1])
                    residual(0)
                if s == GROUPS + 2:
                    second_norm(0)
                    shared_lo([2, 3])
                if 0 <= s - LAG - 1 < GROUPS:
                    normalise(s - LAG - 1)
                if s < GROUPS:
                    maxima(s, range(9, M_BANKS))
                if s == GROUPS:
                    projected(0)
                if s == GROUPS + 2:
                    transposed_lo(0, "X")
                    shared_lo([4, 5])

            def shared_hidden(b, ft):
                name = f"U{b}{ft}"
                dve.wait_ge(post_filled, post.filled(name))
                dve.wait_ge(post_act, post.emptied(f"G{b}{ft}", "A"))
                if ft >= 2 or b:
                    dve.wait_ge(hT_hi_ready, FC * b + ft - 1)
                    dve.wait_ge(hT_lo_ready, FC * b + ft - 1)
                dve.tensor_tensor(h_sb[:, ft % 2, :], ps[:, post.bank(name), :], silu_sb[:, ft % 2, :], ALU.mult) \
                    .then_inc(post_dve, 1)

            def shared_hidden_lo(b, ft):
                dve.wait_ge(hT_hi_ready, FC * b + ft + 1)
                dve.tensor_tensor(hT_lo[:, ft, :], h_sb[:, ft % 2, :], hT_hi[:, ft, :].bitcast(F32), ALU.subtract) \
                    .then_inc(hT_lo_ready, 1)

            def routing():
                e_bc = [P, NT, E]
                dve.wait_ge(post_dve, post.emptied("R1", "D"))
                dve.wait_ge(rconsts_ready, 1)
                dve.tensor_reduce(top[:, :], logits[:, :, :], AX.X, ALU.max).then_inc(top_ready, 1)
                dve.wait_ge(top_ready, 1)
                step(dve.tensor_tensor(hit[:, :, :], logits[:, :, :], top[:, :].unsqueeze(2).to_broadcast(e_bc), ALU.is_equal))
                settle()
                step(dve.tensor_tensor(hit[:, :, :], hit[:, :, :], desc[:, :].unsqueeze(1).to_broadcast(e_bc), ALU.mult))
                settle()
                step(dve.tensor_reduce(first[:, :], hit[:, :, :], AX.X, ALU.max))
                settle()
                step(dve.tensor_tensor(onehot[:, :, :], hit[:, :, :], first[:, :].unsqueeze(2).to_broadcast(e_bc), ALU.is_equal))
                settle()
                dve.tensor_copy(onehot_b[:, :, :], onehot[:, :, :]).then_inc(onehot_ready, 1)

            def slots():
                dve.wait_ge(post_filled, post.filled("RK"))
                bank = ps[:, post.bank("RK"), :]
                ranks = bank[:, 0:NT * E].rearrange("p (t e) -> p t e", e=E)
                counts = bank[:, NT * E:NT * E + E]
                step(dve.tensor_tensor(over[:, :, :], counts.unsqueeze(2).to_broadcast([P, E, E]),
                                       thr[:, :].unsqueeze(1).to_broadcast([P, E, E]), ALU.is_gt))
                settle()
                step(dve.tensor_reduce(n_tiles[:, :], over[:, :, :], AX.X, ALU.add))
                settle()
                step(dve.tensor_tensor_scan(ends[:, :], ones_e[:, :], n_tiles[:, :], 0.0, ALU.mult, ALU.add))
                settle()
                step(dve.tensor_tensor(base_t[:, :], ends[:, :], n_tiles[:, :], ALU.subtract))
                settle()
                dve.scalar_tensor_tensor(out=where[:, :, :], in0=base_t[:, :].unsqueeze(1).to_broadcast([P, NT, E]),
                                         scalar=float(P), in1=ranks, op0=ALU.mult, op1=ALU.add).then_inc(post_dve, 1)
                dve.wait_ge(post_dve, post.emptied("RK", "D"))
                step(dve.tensor_tensor(where[:, :, :], where[:, :, :], onehot[:, :, :], ALU.mult))
                settle()
                step(dve.tensor_reduce(pos_f[:, :], where[:, :, :], AX.X, ALU.add))
                settle()
                dve.tensor_copy(pos_u[:, :], pos_f[:, :]).then_inc(pos_ready, 1)
                step(dve.tensor_tensor(past[:, :, :], ends[:, :].unsqueeze(1).to_broadcast([P, 16, E]),
                                       slot_no[:, :].unsqueeze(2).to_broadcast([P, 16, E]), ALU.is_le))
                settle()
                step(dve.tensor_reduce(own_f[:, :], past[:, :, :], AX.X, ALU.add))
                settle()
                dve.tensor_scalar(own_u[:, :], own_f[:, :], float(E - 1), None, ALU.min).then_inc(owner_ready, 1)
                dve.wait_ge(gate_ready, 1)
                for t in range(NT):
                    dve.tensor_scalar(tok_sb[:, t, :], tok_sb[:, t, :], gate[:, t:t + 1], None, ALU.mult) \
                        .then_inc(gated_ready, 1)

            def shared_units(b, fts):
                for ft in fts:
                    shared_hidden(b, ft)
                    if ft >= 1:
                        shared_hidden_lo(b, ft - 1)
                    if ft == FC - 1:
                        shared_hidden_lo(b, ft)

            take_logits(0)
            shared_units(0, [0])
            transposed_lo(1, "A")
            shared_units(0, [1])
            projected(1)
            shared_units(0, [2])
            residual(1)
            shared_units(0, [3])
            second_norm(1)
            transposed_lo(1, "X")
            take_logits(1)
            routing()
            shared_units(1, [0])
            slots()
            shared_units(1, [1, 2, 3])

            def slot_mul(s):
                name = f"u{s}"
                dve.wait_ge(post_filled, post.filled(name))
                dve.wait_ge(post_act, post.emptied(f"g{s}", "A"))
                if s >= 2:
                    dve.wait_ge(post_filled, post.filled(f"ht{s - 2}"))
                else:
                    dve.wait_ge(hT_lo_ready, NB * FC)
                dve.tensor_tensor(h_sb[:, s % 2, :], ps[:, post.bank(name), :], silu_sb[:, s % 2, :], ALU.mult) \
                    .then_inc(post_dve, 1)

            def take_output(s):
                i, y = s % NT, ysl[:, s % 4, :]
                if s == 0:
                    dve.wait_ge(scattered, 16 * NT)
                if s >= 4:
                    dve.wait_ge(out_scattered[s % 4], 16 * (s // 4))
                dve.wait_ge(ysh_loaded[s % 2], 16 * (s // 2 + 1))
                dve.wait_ge(post_filled, post.filled(f"dn{s}"))
                dve.tensor_tensor(y, ps[:, post.bank(f"dn{s}"), 0:D], ysh_in[:, s % 2, :], ALU.add).then_inc(post_dve, 1)
                dve.wait_ge(post_dve, post.emptied(f"dn{s}", "D"))
                step(dve.bn_stats(stats[:, i, :], y))
                settle()
                step(dve.bn_aggr(mv[:, i, :], stats[:, i, :]))
                settle()
                dve.tensor_scalar(var_e[:, i:i + 1], mv[:, i, 1:2], EPS, None, ALU.add).then_inc(var_ready, 1)

            def last_norm(s):
                i, y = s % NT, ysl[:, s % 4, :]
                dve.wait_ge(rstd_ready, norms + s + 1)
                dve.tensor_scalar(y, y, mv[:, i, 0:1], rstd[:, i:i + 1], ALU.subtract, ALU.mult).then_inc(last_norm_ready, 1)

            def slot_xT_lo(s):
                if s >= 2:
                    dve.wait_ge(post_filled, post.filled(f"u{s - 2}"))
                name = f"xt{s}"
                dve.wait_ge(post_act, post.emptied(name, "A"))
                dve.tensor_tensor(xinT_lo[:, s % 2, :, :].rearrange("p k t -> p (k t)"), ps[:, post.bank(name), 0:KC * P],
                                  xinT_hi[:, s % 2, :, :].rearrange("p k t -> p (k t)").bitcast(F32), ALU.subtract) \
                    .then_inc(post_dve, 1)

            def slot_weights_lo(s, e, half):
                cols = slice(F * half, F * half + F)
                dve.wait_ge(wsl_hi_ready, 2 * s + half + 1)
                dve.tensor_tensor(wsl_lo[s % 2][:, :, cols], owned_half(e, half),
                                  wsl_hi[s % 2][:, :, cols].bitcast(F32), ALU.subtract).then_inc(wsl_lo_ready, 1)

            dve.wait_ge(wgu_loaded, 16 * E)
            dve.wait_ge(owner_ready, 1)
            owners = [owner(s, ENGINE.DVE) for s in range(SLOTS)]
            for s in range(2):
                e = owners[s]
                slot_weights_lo(s, e, 0)
                slot_weights_lo(s, e, 1)
                if s == 0:
                    slot_xT_lo(0)
            slot_mul(0)
            slot_xT_lo(1)
            for s in range(SLOTS):
                if s >= 1:
                    take_output(s - 1)
                if s + 2 < SLOTS:
                    e = owners[s + 2]
                    slot_weights_lo(s + 2, e, 0)
                    slot_xT_lo(s + 2)
                if s >= 1:
                    last_norm(s - 1)
                if s + 1 < SLOTS:
                    slot_mul(s + 1)
                if s + 2 < SLOTS:
                    slot_weights_lo(s + 2, e, 1)
            take_output(SLOTS - 1)
            last_norm(SLOTS - 1)

        @block.tensor
        def _(pe):
            def mm(o, lhsT, rhs, start, stop):
                return pe.matmul(o, lhsT, rhs, start=start, stop=stop)

            def split_mm(o, pairs, start=True, stop=True):
                n, total = 0, 3 * len(pairs)
                for (a_hi, a_lo), (b_hi, b_lo) in pairs:
                    for a, c in ((a_hi, b_hi), (a_hi, b_lo), (a_lo, b_hi)):
                        last = mm(o, a, c, start and n == 0, stop and n == total - 1)
                        n += 1
                return last

            def enter_prep(name):
                prev = prep.before(name)
                if prev:
                    for engine, s in (("A", prep_act), ("D", prep_dve)):
                        if engine in prep.who[prev]:
                            pe.wait_ge(s, prep.emptied(prev, engine))
                return ps[:, prep.bank(name), :]

            pe.wait_ge(consts_ready, 1)
            pe.wait_ge(w_loaded, 64)
            for w in range(3):
                bank = enter_prep(f"W{w}")
                for i in range(4):
                    kc, r = divmod(4 * w + i, 6)
                    last = pe.transpose(bank[:, P * i:P * i + P], wqkv_raw[:, r, kc * P:kc * P + P], ident[:, :])
                last.then_inc(prep_filled, 1)
            bank = enter_prep("WO")
            for i in range(4):
                kc, r = divmod(i, 2)
                last = pe.transpose(bank[:, P * i:P * i + P], wout_raw[:, r, kc * P:kc * P + P], ident[:, :])
            last.then_inc(prep_filled, 1)
            bank = enter_prep("RW")
            for kc in range(KC):
                last = pe.transpose(bank[:, E * kc:E * kc + E], rw_sb[0:E, kc * P:kc * P + P], ident[0:E, 0:E])
            last = pe.transpose(bank[:, KC * E:KC * E + 4], bqk_raw[0:4, :], ident[0:4, 0:4])
            last.then_inc(prep_filled, 1)

            def hl(hi, lo, *index):
                return hi[index], lo[index]

            every = slice(None)
            for b in range(NB):
                toks = slice(S * b, S * b + S)
                pe.wait_ge(norm_ready, TB * (b + 1))
                for kc in range(KC):
                    bank = enter_prep(f"X{b}{kc}")
                    for i in range(TB):
                        last = pe.transpose(bank[:, P * i:P * i + P], tok_sb[:, TB * b + i, kc * P:kc * P + P], ident[:, :])
                    last.then_inc(prep_filled, 1)
                for mt in range(4):
                    bank = enter_prep(f"QK{b}{mt}")
                    pe.wait_ge(prep_dve, prep.emptied(f"X{b}1", "D"))
                    split_mm(bank, [(hl(wT_hi, wT_lo, every, kc, slice(mt * P, mt * P + P)),
                                     hl(tT_hi, tT_lo, every, kc, toks)) for kc in range(KC)]).then_inc(prep_filled, 1)
                for i in range(2):
                    bank = enter_prep(f"V{b}{i}")
                    for n in range(2):
                        t = TB * b + 2 * i + n
                        last = split_mm(bank[:, D * n:D * n + D],
                                        [(hl(tT_hi, tT_lo, every, kc, slice(t * P, t * P + P)),
                                          hl(wT_hi, wT_lo, every, kc, slice(2 * D, 3 * D))) for kc in range(KC)])
                    last.then_inc(prep_filled, 1)
                pe.wait_ge(consts_ready, 3)
                for p in range(8):
                    for name, m, mt in ((f"SQ{b}{p}", 0, p // 4), (f"SK{b}{p}", 2, 2 + p // 4)):
                        bank = enter_prep(name)
                        pe.wait_ge(prep_dve, prep.emptied(f"QK{b}{mt}", "D"))
                        mm(bank, sel[:, m, p % 4, :], qk_hi[:, mt, :], True, False)
                        mm(bank, sel[:, m + 1, p % 4, :], qk_lo[:, mt, :], False, True).then_inc(prep_filled, 1)

            def m_scores(g, banks):
                b, gi = divmod(g, NG)
                for i in banks:
                    heads, qt = m_plan()[i]
                    n = M_BANKS * g + i
                    if m_before(n) is not None:
                        pe.wait_ge(m_reduced, m_before(n) + 1)
                    w = P * (qt + 1)
                    for k, j in enumerate(heads):
                        pair = 2 * gi + j // 2
                        mm(ps[:, m_bank(n), :][:, w * k:w * k + w], q_op[b][:, pair, qt * P:qt * P + P],
                           k_op[b][j % 2][:, pair, 0:w], k == 0, False)
                    for k in range(len(heads)):
                        last = mm(ps[:, m_bank(n), :][:, w * k + w - P:w * k + w], ident_b[:, :], mask2[:, 0, :],
                                  False, k == len(heads) - 1)
                    last.then_inc(m_filled, 1)

            def max_transpose(g):
                pe.wait_ge(m_reduced, M_BANKS * (g + 1))
                if g >= LAG + 1:
                    pe.wait_ge(o_normed, g - LAG)
                pe.transpose(t_ps[0:16, 0:P], rmax[:, g % 2, :], ident[:, :]).then_inc(mT_filled, 1)

            def st_scores(g, u):
                b, gi = divmod(g, NG)
                n = 5 * g + u
                if u == 0:
                    pe.wait_ge(max_placed, 64 * (g + 1))
                if n < 2:
                    pe.wait_ge(m_reduced, M_BANKS * LAG)
                else:
                    pe.wait_ge(exp_done, n - 1)
                opened = set()
                plan = st_plan(u)
                for k, (j, kt, i, c) in enumerate(plan):
                    pair = 2 * gi + j // 2
                    w = S - kt * P
                    closes = all(i2 != i for _, _, i2, _ in plan[k + 1:])
                    last = mm(st_ps[n % 2][:, i, c:c + w], k_op[b][j % 2][:, pair, kt * P:kt * P + P],
                              q_op[b][:, pair, kt * P:S], i not in opened, closes)
                    opened.add(i)
                last.then_inc(st_filled, 1)

            def pv(g, kt, units):
                b, gi = divmod(g, NG)
                pe.wait_ge(causal_done, 5 * g + units)
                if kt == 0 and g >= 1:
                    pe.wait_ge(oT_copied, g)
                for j in range(4):
                    u, c = pt_place(j, kt)
                    w = S - kt * P
                    last = pe.matmul(o_ps[32 * j:32 * j + 32, kt * P:S], v_sb[:, TB * b + kt, 4 * gi + j, :],
                                     pT[:, u, c:c + w], start=kt == 0, stop=kt == 2, tile_position=(0, 32 * j))
                last.then_inc(pv_done, 1)

            def o_transposes(g):
                pe.wait_ge(oT_copied, g + 1)
                pe.wait_ge(mT_dve, min(g + LAG + 1, GROUPS))
                if g >= 1:
                    pe.wait_ge(o_normed, g)
                for qt in range(TB):
                    last = pe.transpose(t_ps[:, P * qt:P * qt + P], oT_sb[:, g % 2, P * qt:P * qt + P], ident[:, :])
                last.then_inc(o_filled, 1)

            pe.wait_ge(prep_dve, prep.emptied("SK17", "D"))
            pe.wait_ge(prep_act, prep.emptied("SK17", "A"))
            def enter_post(name):
                prev = post.before(name)
                if prev:
                    for engine, s in (("A", post_act), ("D", post_dve)):
                        if engine in post.who[prev]:
                            pe.wait_ge(s, post.emptied(prev, engine))
                return ps[:, post.bank(name), :]

            def transposed(b, name):
                for kc in range(KC):
                    bank = enter_post(f"{name}{b}{kc}")
                    for i in range(TB):
                        last = pe.transpose(bank[:, P * i:P * i + P], tok_sb[:, TB * b + i, kc * P:kc * P + P], ident[:, :])
                    last.then_inc(post_filled, 1)

            def out_projection(b):
                for i in range(2):
                    bank = enter_post(f"OP{b}{i}")
                    pe.wait_ge(post_dve, post.emptied(f"A{b}1", "D"))
                    for n in range(2):
                        c = P * (2 * i + n)
                        last = split_mm(bank[:, D * n:D * n + D],
                                        [(hl(rowT_hi[b], rowT_lo[b], every, kc, slice(c, c + P)),
                                          hl(woT_hi, woT_lo, every, kc, every)) for kc in range(KC)])
                    last.then_inc(post_filled, 1)

            def router(b):
                bank = enter_post(f"R{b}")
                pe.wait_ge(post_dve, post.emptied(f"X{b}1", "D"))
                for i in range(TB):
                    last = split_mm(bank[:, E * i:E * i + E],
                                    [(hl(rowT_hi[b], rowT_lo[b], every, kc, slice(i * P, i * P + P)),
                                      hl(rwT_hi, rwT_lo, every, kc, every)) for kc in range(KC)])
                last.then_inc(post_filled, 1)

            for s in range(GROUPS + LAG + 1):
                e, m = s - LAG, s
                on_e, on_m = 0 <= e < GROUPS, m < GROUPS
                if on_e:
                    st_scores(e, 0)
                if on_m:
                    m_scores(m, (0, 1))
                if 0 <= e - 1 < GROUPS:
                    pv(e - 1, 2, 5)
                if 0 <= s - 1 < GROUPS:
                    max_transpose(s - 1)
                if on_m:
                    m_scores(m, (2,))
                if on_e:
                    st_scores(e, 1)
                if s == GROUPS:
                    pe.wait_ge(m_reduced, M_BANKS * GROUPS)
                    transposed(0, "A")
                if on_m:
                    m_scores(m, (3, 4))
                if on_e:
                    st_scores(e, 2)
                    pv(e, 0, 2)
                if on_m:
                    m_scores(m, (5, 6))
                if on_e:
                    st_scores(e, 3)
                if on_m:
                    m_scores(m, (7,))
                if 0 <= e - 1 < GROUPS:
                    o_transposes(e - 1)
                if on_m:
                    m_scores(m, (8,))
                if on_e:
                    st_scores(e, 4)
                if s == GROUPS:
                    out_projection(0)
                if s == GROUPS + 2:
                    pe.wait_ge(norm_ready, TB * NB + TB)
                    transposed(0, "X")
                if on_m:
                    m_scores(m, (9, 10))
                if on_e:
                    pv(e, 1, 4)
                    pv(e, 3, 4)

            def ranks():
                bank = enter_post("RK")
                pe.wait_ge(onehot_ready, 1)
                oh = onehot_b[:, :, :].rearrange("p t e -> p (t e)")
                mm(bank[:, 0:NT * E], lt_b[:, :], oh, True, False)
                for k in range(1, NT):
                    mm(bank[:, E * k:NT * E], ones_b[:, :], oh[:, 0:(NT - k) * E], False, False)
                for k in range(NT):
                    last = mm(bank[:, NT * E:NT * E + E], ones_b[:, :], oh[:, E * k:E * k + E], False, k == NT - 1)
                last.then_inc(post_filled, 1)

            def hidden(b, fts):
                for ft in fts:
                    for name, c in ((f"G{b}{ft}", ft * P), (f"U{b}{ft}", F + ft * P)):
                        bank = enter_post(name)
                        split_mm(bank, [(hl(sgu_hi, sgu_lo, every, kc, slice(c, c + P)),
                                         hl(rowT_hi[b], rowT_lo[b], every, kc, every))
                                        for kc in range(KC)]).then_inc(post_filled, 1)

            def down(b):
                for i in range(2):
                    bank = enter_post(f"DN{b}{i}")
                    pe.wait_ge(hT_lo_ready, FC * (b + 1))
                    for n in range(2):
                        c = P * (2 * i + n)
                        last = split_mm(bank[:, D * n:D * n + D],
                                        [(hl(hT_hi, hT_lo, every, ft, slice(c, c + P)),
                                          hl(sdn_hi, sdn_lo, every, ft, every)) for ft in range(FC)])
                    last.then_inc(post_filled, 1)

            pe.wait_ge(exp_done, 5 * GROUPS)
            router(0)
            pe.wait_ge(sh_lo, 6)
            hidden(0, [0])
            pe.wait_ge(o_normed, GROUPS)
            transposed(1, "A")
            hidden(0, [1])
            out_projection(1)
            hidden(0, [2, 3])
            down(0)
            pe.wait_ge(norm_ready, 2 * TB * NB)
            transposed(1, "X")
            router(1)
            hidden(1, [0])
            ranks()
            hidden(1, [1, 2, 3])
            down(1)

            pe.wait_ge(owner_ready, 1)
            pe.wait_ge(wgu_loaded, 16 * E)
            pe.wait_ge(wdn_loaded, 16 * E)

            def slot_xT(s):
                bank = enter_post(f"xt{s}")
                pe.wait_ge(xin_loaded[s % 5], 16 * (s // 5 + 1))
                for kc in range(KC):
                    last = pe.transpose(bank[:, P * kc:P * kc + P], xin[:, s % 5, D + kc * P:D + kc * P + P], ident[:, :])
                last.then_inc(post_filled, 1)

            def slot_half(s, half):
                name = f"{'gu'[half]}{s}"
                bank = enter_post(name)
                pe.wait_ge(post_dve, post.emptied(f"xt{s}", "D"))
                pe.wait_ge(wsl_lo_ready, 2 * s + half + 1)
                split_mm(bank, [(hl(xinT_hi, xinT_lo, every, s % 2, kc, every),
                                 hl(wsl_hi[s % 2], wsl_lo[s % 2], every, kc, slice(F * half, F * half + F)))
                                for kc in range(KC)]).then_inc(post_filled, 1)

            def slot_hT(s):
                bank = enter_post(f"ht{s}")
                pe.wait_ge(post_dve, post.emptied(f"u{s}", "D"))
                for k in range(FC):
                    last = pe.transpose(bank[:, P * k:P * k + P], h_sb[:, s % 2, P * k:P * k + P], ident[:, :])
                last.then_inc(post_filled, 1)

            def slot_down(s, e):
                bank = enter_post(f"dn{s}")
                pe.wait_ge(post_act, post.emptied(f"ht{s}", "A"))
                for k in range(FC):
                    last = mm(bank[:, 0:D], rhT[:, s % 2, k, :],
                              wdn_sb[:, bass.ds(e * (FC * D) + k * D, D)], k == 0, k == FC - 1)
                last.then_inc(post_filled, 1)

            owners = [owner(s, ENGINE.PE) for s in range(SLOTS)]
            slot_xT(0)
            slot_half(0, 0)
            slot_half(0, 1)
            slot_xT(1)
            for s in range(SLOTS):
                if s + 1 < SLOTS:
                    slot_half(s + 1, 0)
                slot_hT(s)
                if s + 2 < SLOTS:
                    slot_xT(s + 2)
                if s + 1 < SLOTS:
                    slot_half(s + 1, 1)
                slot_down(s, owners[s])


INPUTS = ["L0_attn_x", "L0_attn_Wqkv", "L0_attn_bqkv", "L0_attn_Wout", "L0_attn_bout", "L0_ffn_router_w",
          "L0_ffn_w_gate_up", "L0_ffn_w_down", "L0_ffn_shared_gate_up", "L0_ffn_shared_down"]


def kernel(**inputs):
    import numpy as np
    import concourse.bacc as bacc
    from concourse.bass_utils import run_bass_kernel_spmd

    nc = bacc.Bacc("TRN2", target_bir_lowering=False, num_devices=1)
    arrays, args = {}, []
    for name in INPUTS:
        a = np.ascontiguousarray(inputs[name])
        arrays[name] = a
        args.append(nc.dram_tensor(name, a.shape, mybir.dt.from_np(a.dtype), kind="ExternalInput").ap())
    out = nc.dram_tensor("out", inputs["L0_attn_x"].shape, F32, kind="ExternalOutput").ap()
    build_block(nc, *args, out)
    r = run_bass_kernel_spmd(nc, [arrays], core_ids=[0])
    return r.results[0]["out"]
```

```python
from contextlib import ExitStack

import concourse.bass as bass
from concourse import mybir

ALU = mybir.AluOpType
ACT = mybir.ActivationFunctionType
AX = mybir.AxisListType
F32 = mybir.dt.float32
F32R = mybir.dt.float32r
BF16 = mybir.dt.bfloat16
U32 = mybir.dt.uint32
ENGINE = mybir.EngineType

P = 128
NEG = -1e30
EPS = 1e-5


class Banks:

    def __init__(self, units, turns):
        self.names = [n for n, _ in units]
        self.index = {n: i for i, n in enumerate(self.names)}
        self.who = dict(units)
        self.banks = [banks[i % len(banks)] for count, banks in turns for i in range(count)]
        assert len(self.banks) == len(units)

    def bank(self, name):
        return self.banks[self.index[name]]

    def filled(self, name):
        return self.index[name] + 1

    def emptied(self, name, engine):
        return sum(engine in self.who[n] for n in self.names[: self.index[name] + 1])

    def before(self, name):
        i = self.index[name]
        same = [j for j in range(i) if self.banks[j] == self.banks[i]]
        return self.names[same[-1]] if same else None


def build_block(nc, x, Wqkv, bqkv, Wout, bout, router_w, w_gate_up, w_down, shared_gate_up, shared_down, out):
    NB, S, D = x.shape
    H, HD = 16, 16
    NT = NB * S // P
    TB = S // P
    KC = D // P
    E, _, F2 = w_gate_up.shape
    F = F2 // 2
    FC = F // P
    SLOTS = NT + E - 1
    NG = 4
    SCALE = float(HD) ** -0.5
    assert (D, HD, S, TB, KC, E, F) == (256, 16, 512, 4, 2, 8, 512)

    ctx = ExitStack()
    with ctx:
        def sem(name):
            return ctx.enter_context(nc.semaphore(name))

        BASE = 16544
        KB = 1024

        def at(name, shape, dt, offset):
            return nc.alloc_sbuf_tensor_at(name, shape, dt, offset=BASE + offset)

        ROW = 2 * D + 1
        row_sb = at("row_sb", [P, NT, ROW], F32, -32)
        x_sb = row_sb[:, :, 0:D]
        tok_sb = row_sb[:, :, D:2 * D]
        left_sb = row_sb[:, :, 2 * D]
        tT_hi = at("tT_hi", [P, KC, NT * P], F32R, 16 * KB)
        tT_lo = at("tT_lo", [P, KC, NT * P], F32R, 24 * KB)
        rowT_hi = [at(f"rowT_hi{b}", [P, KC, S], F32R, (188, 16)[b] * KB) for b in range(NB)]
        rowT_lo = [at(f"rowT_lo{b}", [P, KC, S], F32R, (192, 24)[b] * KB) for b in range(NB)]
        q_op = [at(f"q_op{b}", [P, 8, S], F32R, (32 + 32 * b) * KB) for b in range(NB)]
        k_op = [[at(f"k_even{b}", [P, 8, S], F32R, (48 + 32 * b) * KB),
                 at(f"k_odd{b}", [P, 8, S], F32R, (188, 16)[b] * KB)] for b in range(NB)]
        sgu_raw = at("sgu_raw", [P, KC, F2], F32, 32 * KB)
        sgu_lo = at("sgu_lo", [P, KC, F2], F32R, 32 * KB)
        sdn_raw = at("sdn_raw", [P, FC, D], F32, 40 * KB)
        sdn_lo = at("sdn_lo", [P, FC, D], F32R, 40 * KB)
        sgu_hi = at("sgu_hi", [P, KC, F2], F32R, 44 * KB)
        sdn_hi = at("sdn_hi", [P, FC, D], F32R, 52 * KB)
        ysl = at("ysl", [P, 4, D], F32, 0)
        xin = at("xin", [P, 5, ROW], F32, 4 * KB)
        xinT_hi = at("xinT_hi", [P, 2, KC, P], F32R, 48 * KB)
        xinT_lo = at("xinT_lo", [P, 2, KC, P], F32R, 50 * KB)
        wsl_hi = [at(f"wsl_hi{i}", [P, KC, F2], F32R, (16, 24)[i] * KB) for i in range(2)]
        wsl_lo = [at(f"wsl_lo{i}", [P, KC, F2], F32R, (32, 56)[i] * KB) for i in range(2)]
        ysh_in = at("ysh_in", [P, 2, D], F32, 52 * KB)
        bo_bc = at("bo_bc", [P, D], F32, 63 * KB)
        wdn_sb = at("wdn_sb", [P, E * FC * D], F32, 64 * KB)
        v_sb = at("v_sb", [P, NT, H, 32], F32, 96 * KB)
        pT = at("pT", [P, 5, 1024], F32, 112 * KB)
        oT_sb = at("oT_sb", [P, 2, S], F32, 132 * KB)
        ysh_sb = at("ysh_sb", [P, NT, D], F32, 96 * KB)
        hT_hi = at("hT_hi", [P, FC, S], F32R, 104 * KB)
        hT_lo = at("hT_lo", [P, FC, S], F32R, 112 * KB)
        silu_sb = at("silu_sb", [P, 2, S], F32, 120 * KB)
        h_sb = at("h_sb", [P, 2, S], F32, 124 * KB)
        rhT = at("rhT", [P, 2, FC, P], F32, 128 * KB)
        woT_hi = at("woT_hi", [P, KC, D], F32R, 136 * KB)
        woT_lo = at("woT_lo", [P, KC, D], F32R, 138 * KB)
        wgu_sb = at("wgu_sb", [P, E * KC * F2], F32, 140 * KB)
        wqkv_raw = at("wqkv_raw", [P, 6, D], F32, 140 * KB)
        wout_raw = at("wout_raw", [P, 2, D], F32, 146 * KB)
        wT_hi = at("wT_hi", [P, KC, 3 * D], F32R, 148 * KB)
        wT_lo = at("wT_lo", [P, KC, 3 * D], F32R, 154 * KB)
        qk_hi = at("qk_hi", [P, 4, S], F32R, 160 * KB)
        qk_lo = at("qk_lo", [P, 4, S], F32R, 168 * KB)
        sel = at("sel", [P, 4, 4, P], F32R, 176 * KB)
        zero_sb = at("zero_sb", [P, ROW], F32, 112 * KB)
        bv_bc = at("bv_bc", [P, D], F32, 185 * KB)
        rw_sb = at("rw_sb", [P, D], F32, 186 * KB)
        bqk_raw = at("bqk_raw", [P, P], F32, 187 * KB)
        small = [204 * KB]

        def little(name, shape, dt, size):
            t = at(name, shape, dt, small[0])
            n = size
            for k in shape[1:]:
                n *= k
            small[0] += (n + 31) // 32 * 32
            return t

        ident = little("ident", [P, P], F32, 4)
        ident_b = little("ident_b", [P, P], BF16, 2)
        mask = little("mask", [P, P], BF16, 2)
        mT_hi = little("mT_hi", [16, P], F32R, 4)
        mT_lo = little("mT_lo", [16, P], F32R, 4)
        bqk = little("bqk", [P, 4], F32, 4)
        k_rows = little("k_rows", [P, 2], F32, 4)
        k_ones = little("k_ones", [P, 2], F32, 4)
        stats = little("stats", [P, NT, 6], F32, 4)
        mv = little("mv", [P, NT, 2], F32, 4)
        var_e = little("var_e", [P, NT], F32, 4)
        rstd = little("rstd", [P, NT], F32, 4)
        shift = little("shift", [P, NT], F32, 4)
        mhalf = little("mhalf", [P, NT], F32, 4)
        rwT = little("rwT", [P, KC, 2, E], F32R, 4)
        rmax = little("rmax", [P, 2, 16], F32, 4)
        orec = little("orec", [P, 16], F32, 4)
        assert BASE + small[0] <= 229344, small[0]
        small[0] = 132 * KB
        lt_b = little("lt_b", [P, P], BF16, 2)
        ones_b = little("ones_b", [P, P], BF16, 2)
        logits = little("logits", [P, NT, E], F32, 4)
        top = little("top", [P, NT], F32, 4)
        hit = little("hit", [P, NT, E], F32, 4)
        onehot = little("onehot", [P, NT, E], F32, 4)
        onehot_b = little("onehot_b", [P, NT, E], BF16, 2)
        first = little("first", [P, NT], F32, 4)
        gate = little("gate", [P, NT], F32, 4)
        desc = little("desc", [P, E], F32, 4)
        thr = little("thr", [P, E], F32, 4)
        slot_no = little("slot_no", [P, 16], F32, 4)
        over = little("over", [P, E, E], F32, 4)
        n_tiles = little("n_tiles", [P, E], F32, 4)
        ones_e = little("ones_e", [P, E], F32, 4)
        ends = little("ends", [P, E], F32, 4)
        base_t = little("base_t", [P, E], F32, 4)
        where = little("where", [P, NT, E], F32, 4)
        pos_f = little("pos_f", [P, NT], F32, 4)
        pos_u = little("pos_u", [P, NT], U32, 4)
        past = little("past", [P, 16, E], F32, 4)
        own_f = little("own_f", [P, 16], F32, 4)
        dest_u = little("dest_u", [P, 16], U32, 4)
        own_u = little("own_u", [P, 16], U32, 4)
        assert small[0] <= 136 * KB, small[0]

        ps = ctx.enter_context(nc.psum_tensor("ps", [P, 8, 512], F32))
        st_ps = [ps[:, 2 * i:2 * i + 2, :] for i in range(2)]
        m_ps = [ps[:, 4 + i, :] for i in range(2)]
        o_ps = ps[:, 6, :]
        t_ps = ps[:, 7, :]

        xs_dram = nc.dram_tensor("xs_dram", (SLOTS * P, ROW), F32).ap()
        ysh_dram = nc.dram_tensor("ysh_dram", (SLOTS * P, D), F32).ap()

        x_loaded = [sem(f"x_loaded{b}") for b in range(NB)]
        w_loaded = sem("w_loaded")
        bias_loaded = sem("bias_loaded")
        bo_loaded = sem("bo_loaded")
        wgu_loaded = sem("wgu_loaded")
        wdn_loaded = sem("wdn_loaded")
        shared_loaded = sem("shared_loaded")
        slots_zeroed = sem("slots_zeroed")
        pool_step = sem("pool_step")
        dve_step = sem("dve_step")
        consts_ready = sem("consts_ready")
        rconsts_ready = sem("rconsts_ready")
        zero_ready = sem("zero_ready")
        var_ready = sem("var_ready")
        rstd_ready = sem("rstd_ready")
        shift_ready = sem("shift_ready")
        act_normed = sem("act_normed")
        norm_ready = sem("norm_ready")
        prep_filled = sem("prep_filled")
        prep_act = sem("prep_act")
        prep_dve = sem("prep_dve")
        m_filled = sem("m_filled")
        m_reduced = sem("m_reduced")
        mT_filled = sem("mT_filled")
        mT_act = sem("mT_act")
        mT_dve = sem("mT_dve")
        max_placed = sem("max_placed")
        st_filled = sem("st_filled")
        exp_done = sem("exp_done")
        causal_done = sem("causal_done")
        pv_done = sem("pv_done")
        oT_copied = sem("oT_copied")
        o_filled = sem("o_filled")
        o_normed = sem("o_normed")
        sh_hi = sem("sh_hi")
        sh_lo = sem("sh_lo")
        post_filled = sem("post_filled")
        post_act = sem("post_act")
        post_dve = sem("post_dve")
        hT_hi_ready = sem("hT_hi_ready")
        hT_lo_ready = sem("hT_lo_ready")
        onehot_ready = sem("onehot_ready")
        top_ready = sem("top_ready")
        gate_ready = sem("gate_ready")
        gated_ready = sem("gated_ready")
        pos_ready = sem("pos_ready")
        owner_ready = sem("owner_ready")
        scattered = sem("scattered")
        wsl_hi_ready = sem("wsl_hi_ready")
        wsl_lo_ready = sem("wsl_lo_ready")
        ysh_scattered = sem("ysh_scattered")
        xin_loaded = [sem(f"xin_loaded{i}") for i in range(5)]
        ysh_loaded = [sem(f"ysh_loaded{i}") for i in range(2)]
        last_norm_ready = sem("last_norm_ready")
        final_ready = sem("final_ready")
        out_scattered = [sem(f"out_scattered{i}") for i in range(4)]

        LAG = 3
        M_BANKS = 11

        def qk_units(b, mts):
            return [(f"QK{b}{mt}", "AD") for mt in mts]

        def v_units(b):
            return [(f"V{b}{i}", "D") for i in range(2)]

        def op_units(b, pairs, alone=False):
            return [u for p in pairs for u in ((f"SQ{b}{p}", "D" if p % 2 and not alone else "A"),
                                               (f"SK{b}{p}", "A" if alone else "AD"))]

        x_units = [[(f"X{b}{kc}", "AD") for kc in range(KC)] for b in range(NB)]
        first_units = [(f"W{i}", "AD") for i in range(3)] + [("WO", "AD"), ("RW", "AD")]
        first_units += x_units[0] + qk_units(0, range(4)) + v_units(0) + x_units[1] + op_units(0, (0, 1))
        n_in_eight = len(first_units)
        first_units += v_units(1)
        mixed_units = [op_units(0, (2, 3), True) + qk_units(1, (0, 2)) + op_units(0, (4, 5), True),
                       op_units(0, (6, 7), True) + qk_units(1, (1, 3)) + op_units(1, (0, 1, 2), True),
                       op_units(1, (3, 4)) + op_units(1, (5, 6, 7), True)]
        assert len(mixed_units) == LAG
        prep_units = first_units + [u for units in mixed_units for u in units]
        prep = Banks(prep_units, [(n_in_eight, range(8)), (len(prep_units) - n_in_eight, (0, 1, 2, 3, 6))])
        LAST_PREP = prep_units[-1][0]

        def mixed(g, i):
            units = mixed_units[g]
            return [name for name, _ in units[len(units) * i // M_BANKS:len(units) * (i + 1) // M_BANKS]]

        def attn_out_units(b):
            return [(f"A{b}{kc}", "AD") for kc in range(KC)] + [(f"OP{b}{i}", "D") for i in range(2)]

        def router_units(b):
            return [(f"X{b}{kc}", "AD") for kc in range(KC)] + [(f"R{b}", "D")]

        def hidden_units(b, fts):
            return [(f"{n}{b}{ft}", who) for ft in fts for n, who in (("G", "A"), ("U", "D"))]

        def down_units(b):
            return [(f"DN{b}{i}", "A") for i in range(2)]

        post_units = attn_out_units(0) + router_units(0)
        n_early = len(post_units)
        post_units += attn_out_units(1)[:2] + hidden_units(0, [0]) + attn_out_units(1)[2:]
        post_units += hidden_units(0, [1, 2, 3]) + down_units(0)[:1] + router_units(1)[:KC]
        post_units += down_units(0)[1:] + router_units(1)[KC:]
        post_units += hidden_units(1, [0])[:1] + [("RK", "D")] + hidden_units(1, [0])[1:]
        post_units += hidden_units(1, [1, 2, 3]) + down_units(1)
        post_units += [("xt0", "AD"), ("g0", "A"), ("u0", "D"), ("xt1", "AD")]
        for s in range(SLOTS):
            if s + 1 < SLOTS:
                post_units += [(f"g{s + 1}", "A")]
            post_units += [(f"ht{s}", "A")]
            if s + 2 < SLOTS:
                post_units += [(f"xt{s + 2}", "AD")]
            if s + 1 < SLOTS:
                post_units += [(f"u{s + 1}", "D")]
            post_units += [(f"dn{s}", "D")]
        post = Banks(post_units, [(n_early, (4, 5)), (len(post_units) - n_early, range(8))])

        GROUPS = NB * NG

        def m_plan():
            return [([0], 3), ([1], 3), ([2], 3), ([3], 3), ([0], 2), ([1], 2), ([2], 2), ([3], 2),
                    ([0, 2], 1), ([1, 3], 1), ([0, 2, 1, 3], 0)]

        def st_plan(u):
            if u < 2:
                return [(2 * u + i, 0, i, 0) for i in range(2)]
            if u < 4:
                return [(2 * (u - 2) + i, kt, i, c) for i in range(2) for kt, c in ((3, 0), (1, P))]
            return [(2 * i + k, 2, i, 256 * k) for i in range(2) for k in range(2)]

        def pt_place(j, kt):
            for u in range(5):
                for j2, kt2, i, c in st_plan(u):
                    if (j2, kt2) == (j, kt):
                        return u, 512 * i + c

        def slot_owners(engine):
            return nc.values_load_multi_w_load_instructions(
                own_u[0:1, 0:SLOTS], engines=(engine,), min_val=0, max_val=E - 1,
                skip_runtime_bounds_check_because="own_u is clamped to 0..E-1 when it is written")[1]

        def owned_half(e, half):
            return wgu_sb[:, bass.ds(e * (KC * F2), KC * F2)].rearrange("p (k n) -> p k n", k=KC)[:, :, F * half:F * half + F]

        MT_ORDER = [2 * (j % 2) + j // 2 for j in range(4)]

        block = ctx.enter_context(nc.Block())

        def row_broadcast(ap, lo, n):
            return bass.AP(tensor=ap.tensor, offset=lo, ap=[[0, P], [1, n]])

        @block.sync
        def _(sp):
            for b in range(NB):
                sp.dma_start(x_sb[:, TB * b:TB * b + TB, :], x[b].rearrange("(t p) d -> p t d", p=P)) \
                    .then_inc(x_loaded[b], 16)
            sp.wait_ge(x_loaded[1], 16)
            sp.wait_ge(w_loaded, 64)
            sp.wait_ge(zero_ready, 1)
            for rows, width in ((xs_dram, ROW), (ysh_dram, D)):
                sp.dma_start(rows.rearrange("(s p) d -> p s d", p=P),
                             zero_sb[:, 0:width].unsqueeze(1).to_broadcast([P, SLOTS, width])).then_inc(slots_zeroed, 16)
            wgu_v = wgu_sb[:, :].rearrange("p (e k n) -> p e k n", e=E, k=KC)

            def load_wgu(experts):
                for e in experts:
                    sp.dma_start(wgu_v[:, e, :, :], w_gate_up[e].rearrange("(k p) n -> p k n", p=P)).then_inc(wgu_loaded, 16)

            for g in range(GROUPS):
                b, gi = divmod(g, NG)
                sp.wait_ge(mT_act, g + 1)
                sp.wait_ge(mT_dve, g + 1)
                for par in range(2):
                    for row, src in ((48, mT_hi), (49, mT_lo)):
                        r = 64 * par + row
                        dst = q_op[b][r:r + 1, 2 * gi:2 * gi + 2, :].bitcast(F32)
                        sp.dma_start(dst.rearrange("o j (t k) -> o (j t) k", k=P),
                                     src[8 * par:8 * par + 8, :].bitcast(F32)).then_inc(max_placed, 16)
                if g == LAG - 1:
                    sp.wait_ge(prep_filled, len(prep_units))
                    sp.wait_ge(prep_dve, prep.emptied(LAST_PREP, "D"))
                    sp.wait_ge(prep_act, prep.emptied(LAST_PREP, "A"))
                if LAG - 1 <= g < LAG + 2:
                    load_wgu((2 * (g - LAG + 1), 2 * (g - LAG + 1) + 1))
                if g == 5:
                    sp.wait_ge(st_filled, 5 * NG)
                    sp.dma_start(sgu_raw[:, :, :], shared_gate_up.rearrange("(k p) n -> p k n", p=P)).then_inc(shared_loaded, 16)
                    sp.dma_start(sdn_raw[:, :, :], shared_down.rearrange("(k p) n -> p k n", p=P)).then_inc(shared_loaded, 16)
                    load_wgu((E - 1,))
                    sp.dma_start(bo_bc[:, :], row_broadcast(bout, 0, D)).then_inc(bo_loaded, 16)
            sp.wait_ge(st_filled, 5 * GROUPS)
            wdn_v = wdn_sb[:, :].rearrange("p (e k n) -> p e k n", e=E, k=FC)
            for e in range(E):
                sp.dma_start(wdn_v[:, e, :, :], w_down[e].rearrange("(k p) n -> p k n", p=P)).then_inc(wdn_loaded, 16)
            sp.wait_ge(post_filled, post.filled("U03"))
            load_wgu((E - 2,))
            sp.wait_ge(scattered, 16 * NT)

            def load_rows(s):
                if s >= 5:
                    sp.wait_ge(final_ready, s - 4)
                sp.dma_start(xin[:, s % 5, :], xs_dram[s * P:s * P + P, :]).then_inc(xin_loaded[s % 5], 16)

            def load_shared(s):
                if s >= 2:
                    sp.wait_ge(post_dve, post.emptied(f"dn{s - 2}", "D"))
                sp.dma_start(ysh_in[:, s % 2, :], ysh_dram[s * P:s * P + P, :]).then_inc(ysh_loaded[s % 2], 16)

            for s in range(5):
                load_rows(s)
            sp.wait_ge(ysh_scattered, 16 * NT)
            for s in range(2):
                load_shared(s)
            for s in range(SLOTS):
                if s + 2 < SLOTS:
                    load_shared(s + 2)
                if s + 5 < SLOTS:
                    load_rows(s + 5)

        @block.gpsimd
        def _(pool):
            steps = 0

            def step(ins):
                nonlocal steps
                steps += 1
                ins.then_inc(pool_step, 1)

            step(pool.memset(ident[:, :], 0.0))
            step(pool.memset(mhalf[:, :], -0.5))
            pool.memset(zero_sb[:, :], 0.0).then_inc(zero_ready, 1)
            pool.wait_ge(pool_step, steps)
            step(pool.affine_select(out=ident[:, :], in_=ident[:, :], compare_op=ALU.not_equal, fill=1.0,
                                    base=0, pattern=[[-1, P]], channel_multiplier=1))
            pool.wait_ge(pool_step, steps)
            pool.memset(k_ones[:, :], 0.0).then_inc(consts_ready, 1)

            norms = 0

            def rstd_of(tiles):
                nonlocal norms
                norms += 1
                pool.wait_ge(var_ready, norms)
                pool.tensor_tensor(rstd[:, tiles], var_e[:, tiles], mhalf[:, tiles], ALU.pow).then_inc(rstd_ready, 1)

            rstd_of(slice(0, TB))
            pool.iota(left_sb, [[-P, NT]], base=NT * P, channel_multiplier=-1,
                      allow_small_or_imprecise_dtypes=True).then_inc(consts_ready, 1)
            step(pool.memset(sel[:, :, :, :].bitcast(F32), 0.0))
            step(pool.memset(mask[:, :], 0.0))
            step(pool.memset(ident_b[:, :], 0.0))
            step(pool.memset(k_rows[:, :], 1.0))
            step(pool.memset(v_sb[:, :, :, 16:32], 1.0))
            pool.wait_ge(pool_step, steps)
            sel_v = sel[:, :, :, :].rearrange("p m h (r x) -> p m (h r) x", r=2)
            for m, part in ((0, 0), (0, 2), (1, 1), (2, 0), (2, 1), (3, 2)):
                view = sel_v[:, m, :, 16 * part:16 * part + 16]
                step(pool.affine_select(out=view, in_=view.bitcast(F32), compare_op=ALU.not_equal, fill=1.0,
                                        base=0, pattern=[[-16, 8], [-1, 16]], channel_multiplier=1))
            step(pool.affine_select(out=ident_b[:, :], in_=ident_b[:, :], compare_op=ALU.not_equal, fill=1.0,
                                    base=0, pattern=[[-1, P]], channel_multiplier=1))
            step(pool.affine_select(out=mask[:, :], in_=mask[:, :], compare_op=ALU.is_ge, fill=NEG,
                                    base=0, pattern=[[-1, P]], channel_multiplier=1))
            step(pool.affine_select(out=k_rows[:, 0:1], in_=k_rows[:, 0:1], compare_op=ALU.is_ge, fill=0.0,
                                    base=63, pattern=[[0, 1]], channel_multiplier=-1))
            step(pool.affine_select(out=k_rows[:, 1:2], in_=k_rows[:, 1:2], compare_op=ALU.is_ge, fill=0.0,
                                    base=-64, pattern=[[0, 1]], channel_multiplier=1))
            for r in (48, 49):
                pool.wait_ge(pool_step, steps)
                step(pool.affine_select(out=k_ones[:, :], in_=k_ones[:, :], compare_op=ALU.not_equal, fill=1.0,
                                        base=-r, pattern=[[-64, 2]], channel_multiplier=1))
            pool.wait_ge(pool_step, steps)
            pool.memset(rmax[:, :, :], 0.0).then_inc(consts_ready, 1)
            rstd_of(slice(TB, 2 * TB))

            def causal(g, u):
                pool.wait_ge(exp_done, 5 * g + u + 1)
                if u < 2:
                    view = pT[:, u, :].rearrange("p (i c) -> p i c", i=2)[:, :, 0:P]
                    pattern = [[0, 2], [1, P]]
                elif u < 4:
                    view = pT[:, u, :].rearrange("p (i c) -> p i c", i=2)[:, :, 0:2 * P]
                    pattern = [[0, 2], [0, 2], [1, P]]
                else:
                    view = pT[:, u, :].rearrange("p (i c) -> p i c", i=4)[:, :, 0:P]
                    pattern = [[0, 4], [1, P]]
                pool.affine_select(out=view, in_=view, compare_op=ALU.is_ge, fill=0.0, base=0,
                                   pattern=pattern, channel_multiplier=-1).then_inc(causal_done, 1)

            for s in range(LAG, GROUPS + LAG):
                for u in range(5):
                    causal(s - LAG, u)
                    if (s, u) in ((GROUPS + 1, 1), (GROUPS + 2, 0)):
                        rstd_of(slice(0, TB))
            pool.wait_ge(o_filled, GROUPS)
            step(pool.memset(lt_b[:, :], 1.0))
            step(pool.memset(ones_b[:, :], 1.0))
            step(pool.memset(ones_e[:, :], 1.0))
            step(pool.iota(desc[:, :], [[-1, E]], base=E, channel_multiplier=0, allow_small_or_imprecise_dtypes=True))
            step(pool.iota(thr[:, :], [[P, E]], base=0, channel_multiplier=0, allow_small_or_imprecise_dtypes=True))
            step(pool.iota(slot_no[:, :], [[1, 16]], base=0, channel_multiplier=0, allow_small_or_imprecise_dtypes=True))
            pool.wait_ge(pool_step, steps)
            pool.affine_select(out=lt_b[:, :], in_=lt_b[:, :], compare_op=ALU.is_gt, fill=0.0, base=0,
                               pattern=[[1, P]], channel_multiplier=-1).then_inc(rconsts_ready, 1)
            rstd_of(slice(TB, 2 * TB))
            rstd_of(slice(TB, 2 * TB))
            pool.wait_ge(slots_zeroed, 32)
            pool.wait_ge(pos_ready, 1)
            for t in range(NT):
                pool.wait_ge(gated_ready, t + 1)
                pool.indirect_dma_start(xs_dram, bass.IndirectOffsetOnAxis(pos_u[:, t:t + 1], 0),
                                        row_sb[:, t, :], None).then_inc(scattered, 16)
            pool.wait_ge(xin_loaded[1], 16)
            for t in range(NT):
                pool.wait_ge(post_act, post.emptied(f"DN{t // TB}{t % TB // 2}", "A"))
                pool.indirect_dma_start(ysh_dram, bass.IndirectOffsetOnAxis(pos_u[:, t:t + 1], 0),
                                        ysh_sb[:, t, :], None).then_inc(ysh_scattered, 16)
            out_rows = out.rearrange("b s d -> (b s) d")
            for s in range(SLOTS):
                i, y, rows = s % NT, ysl[:, s % 4, :], xin[:, s % 5, :]
                pool.wait_ge(xin_loaded[s % 5], 16 * (s // 5 + 1))
                step(pool.tensor_scalar(dest_u[:, s:s + 1], rows[:, 2 * D:ROW], -1.0, float(NT * P), ALU.mult, ALU.add))
                rstd_of(slice(i, i + 1))
                pool.wait_ge(last_norm_ready, s + 1)
                pool.tensor_tensor(y, y, rows[:, 0:D], ALU.add).then_inc(final_ready, 1)
                pool.wait_ge(final_ready, s + 1)
                pool.indirect_dma_start(out_rows, bass.IndirectOffsetOnAxis(dest_u[:, s:s + 1], 0), ysl[:, s % 4, :], None,
                                        bounds_check=NT * P - 1, oob_is_err=False).then_inc(out_scattered[s % 4], 16)
            for i in range(4):
                pool.wait_ge(out_scattered[i], 16 * ((SLOTS - i + 3) // 4))

        @block.scalar
        def _(act):
            act.dma_start(wqkv_raw[:, :, :], Wqkv.rearrange("(r p) d -> p r d", p=P)).then_inc(w_loaded, 16)
            act.dma_start(wout_raw[:, :, :], Wout.rearrange("(r p) d -> p r d", p=P)).then_inc(w_loaded, 16)
            act.dma_start(rw_sb[0:E, :], router_w).then_inc(w_loaded, 16)
            act.dma_start(bqk_raw[0:4, :], bqkv[0:2 * D].rearrange("(m p) -> m p", p=P)).then_inc(w_loaded, 16)
            act.dma_start(bv_bc[:, :], row_broadcast(bqkv, 2 * D, D)).then_inc(bias_loaded, 16)

            def prep_unit(name, out_ap, in_ap, **kw):
                act.wait_ge(prep_filled, prep.filled(name))
                act.activation(out_ap, in_ap, ACT.Identity if kw else ACT.Copy, **kw).then_inc(prep_act, 1)

            wT_f = wT_hi[:, :, :].rearrange("p k n -> p (k n)")
            for i in range(3):
                prep_unit(f"W{i}", wT_f[:, 512 * i:512 * i + 512], ps[:, prep.bank(f"W{i}"), :])
            prep_unit("WO", woT_hi[:, :, :].rearrange("p k n -> p (k n)"), ps[:, prep.bank("WO"), :])
            act.wait_ge(prep_filled, prep.filled("RW"))
            act.activation(bqk[:, :], ps[:, prep.bank("RW"), KC * E:KC * E + 4], ACT.Copy).then_inc(bias_loaded, 1)
            prep_unit("RW", rwT[:, :, 0, :], ps[:, prep.bank("RW"), 0:KC * E].rearrange("p (k e) -> p k e", k=KC))
            act.wait_ge(bias_loaded, 17)

            def prepare(name):
                kind, b, i = name[:-2], int(name[-2]), int(name[-1])
                bank = ps[:, prep.bank(name), :]
                if kind == "X":
                    prep_unit(name, tT_hi[:, i, S * b:S * b + S], bank)
                if kind == "QK":
                    prep_unit(name, qk_hi[:, i, :], bank, bias=bqk[:, i:i + 1])
                if kind == "SQ" and prep.who[name] == "A":
                    prep_unit(name, q_op[b][:, i, :], bank)
                if kind == "SK":
                    act.wait_ge(prep_filled, prep.filled(name))
                    if prep.who[name] == "A":
                        act.activation(k_op[b][1][:, i, :], bank, ACT.Identity, bias=k_ones[:, 1:2], scale=k_rows[:, 1:2])
                    prep_unit(name, k_op[b][0][:, i, :], bank, bias=k_ones[:, 0:1], scale=k_rows[:, 0:1])

            for name, _ in first_units[5:]:
                if name == "SQ00":
                    act.wait_ge(consts_ready, 3)
                prepare(name)

            def exps(g, u):
                n = 5 * g + u
                act.wait_ge(st_filled, n + 1)
                if n == 0:
                    act.wait_ge(slots_zeroed, 32)
                if g >= 1:
                    act.wait_ge(pv_done, 4 * (g - 1) + (1, 1, 3, 3, 4)[u])
                act.activation(pT[:, u, :], st_ps[n % 2].rearrange("p i c -> p (i c)"), ACT.Exp, scale=SCALE) \
                    .then_inc(exp_done, 1)

            def oT_copy(g):
                act.wait_ge(pv_done, 4 * g + 4)
                if g >= 2:
                    act.wait_ge(o_filled, g - 1)
                act.activation(oT_sb[:, g % 2, :], o_ps, ACT.Copy).then_inc(oT_copied, 1)

            def max_hi(g):
                act.wait_ge(mT_filled, g + 1)
                if g >= 1:
                    act.wait_ge(max_placed, 64 * g)
                act.activation(mT_hi[:, :], t_ps[0:16, 0:P], ACT.Copy, scale=-1.0).then_inc(mT_act, 1)

            def shared_hi(cs):
                for c in cs:
                    act.wait_ge(shared_loaded, 32)
                    if c < 4:
                        k, half = divmod(c, 2)
                        o, r = (w[:, k, 512 * half:512 * half + 512] for w in (sgu_hi, sgu_raw))
                    else:
                        o, r = (w[:, 2 * (c - 4):2 * (c - 4) + 2, :] for w in (sdn_hi, sdn_raw))
                    act.activation(o, r, ACT.Copy).then_inc(sh_hi, 1)

            def post_unit(name, out_ap, in_ap, func=ACT.Copy):
                act.wait_ge(post_filled, post.filled(name))
                return act.activation(out_ap, in_ap, func).then_inc(post_act, 1)

            def transposed_hi(b, name):
                for kc in range(KC):
                    post_unit(f"{name}{b}{kc}", rowT_hi[b][:, kc, :], ps[:, post.bank(f"{name}{b}{kc}"), :])

            for s in range(LAG):
                for i in range(M_BANKS):
                    for name in mixed(s, i):
                        prepare(name)
                    if s >= 1 and i == 2:
                        max_hi(s - 1)
            for s in range(LAG, GROUPS + LAG + 1):
                e = s - LAG
                if 0 <= e < GROUPS:
                    exps(e, 0)
                if 0 <= s - 1 < GROUPS:
                    max_hi(s - 1)
                if 0 <= e < GROUPS:
                    exps(e, 1)
                if 0 <= e - 1 < GROUPS:
                    oT_copy(e - 1)
                if 0 <= e < GROUPS:
                    if s == GROUPS:
                        transposed_hi(0, "A")
                    for u in range(2, 5):
                        exps(e, u)
                if s == GROUPS + 2:
                    transposed_hi(0, "X")
                if GROUPS <= s < GROUPS + 3:
                    shared_hi([2 * (s - GROUPS), 2 * (s - GROUPS) + 1])


            def shared_hidden(b, ft):
                post_unit(f"G{b}{ft}", silu_sb[:, ft % 2, :], ps[:, post.bank(f"G{b}{ft}"), :], ACT.Silu)

            def shared_hidden_hi(b, ft):
                act.wait_ge(post_dve, post.emptied(f"U{b}{ft}", "D"))
                if b == 1:
                    act.wait_ge(post_filled, post.filled("DN01"))
                act.activation(hT_hi[:, ft, :], h_sb[:, ft % 2, :], ACT.Copy).then_inc(hT_hi_ready, 1)

            def shared_units(b, fts):
                for ft in fts:
                    if b or ft >= 2:
                        bb, ff = (b, ft - 2) if ft >= 2 else (b - 1, ft + 2)
                        act.wait_ge(post_dve, post.emptied(f"U{bb}{ff}", "D"))
                    shared_hidden(b, ft)
                    if ft >= 1:
                        shared_hidden_hi(b, ft - 1)
                    if ft == FC - 1:
                        shared_hidden_hi(b, ft)

            def shared_down(b, i):
                name = f"DN{b}{i}"
                post_unit(name, ysh_sb[:, TB * b + 2 * i:TB * b + 2 * i + 2, :].rearrange("p t d -> p (t d)"),
                          ps[:, post.bank(name), :])

            def apply_norm(dst, src, tiles, n):
                act.wait_ge(shift_ready, n)
                for t in tiles:
                    act.activation(dst[:, t, :], src[:, t, :], ACT.Identity, bias=shift[:, t:t + 1], scale=rstd[:, t:t + 1]) \
                        .then_inc(act_normed, 1)

            transposed_hi(1, "A")
            shared_units(0, [0, 1, 2])
            apply_norm(tok_sb, tok_sb, range(TB, 2 * TB), 1)
            shared_units(0, [3])
            apply_norm(tok_sb, x_sb, range(TB + 2, 2 * TB), 2)
            shared_down(0, 0)
            transposed_hi(1, "X")
            shared_down(0, 1)
            act.wait_ge(top_ready, 1)
            act.activation(gate[:, :], top[:, :], ACT.Sigmoid).then_inc(gate_ready, 1)
            shared_units(1, [0, 1, 2, 3])

            def slot_xT(s):
                if s >= 2:
                    act.wait_ge(post_filled, post.filled(f"u{s - 2}"))
                post_unit(f"xt{s}", xinT_hi[:, s % 2, :, :].rearrange("p k t -> p (k t)"),
                          ps[:, post.bank(f"xt{s}"), 0:KC * P])

            def slot_silu(s):
                if s >= 2:
                    act.wait_ge(post_dve, post.emptied(f"u{s - 2}", "D"))
                else:
                    act.wait_ge(post_dve, post.emptied(f"U1{FC - 2 + s}", "D"))
                post_unit(f"g{s}", silu_sb[:, s % 2, :], ps[:, post.bank(f"g{s}"), :], ACT.Silu)

            def slot_weights(s, e, half):
                act.wait_ge(post_filled, post.filled(f"{'gu'[half]}{s - 2}" if s >= 2 else f"U1{FC - 1}"))
                act.activation(wsl_hi[s % 2][:, :, F * half:F * half + F], owned_half(e, half), ACT.Copy) \
                    .then_inc(wsl_hi_ready, 1)

            def slot_hT(s):
                if s >= 2:
                    act.wait_ge(post_filled, post.filled(f"dn{s - 2}"))
                post_unit(f"ht{s}", rhT[:, s % 2, :, :].rearrange("p k t -> p (k t)"), ps[:, post.bank(f"ht{s}"), :])

            act.wait_ge(owner_ready, 1)
            act.wait_ge(wgu_loaded, 16 * E)
            owners = slot_owners(ENGINE.Activation)
            for s in range(2):
                e = owners[s]
                slot_weights(s, e, 0)
                slot_weights(s, e, 1)
                if s == 0:
                    shared_down(1, 0)
                    shared_down(1, 1)
            slot_xT(0)
            slot_silu(0)
            slot_xT(1)
            for s in range(SLOTS):
                if s + 2 < SLOTS:
                    e = owners[s + 2]
                    slot_weights(s + 2, e, 0)
                if s + 1 < SLOTS:
                    slot_silu(s + 1)
                slot_hT(s)
                if s + 2 < SLOTS:
                    slot_xT(s + 2)
                    slot_weights(s + 2, e, 1)

        @block.vector
        def _(dve):
            steps = 0

            def step(ins):
                nonlocal steps
                steps += 1
                return ins.then_inc(dve_step, 1)

            def settle():
                dve.wait_ge(dve_step, steps)

            norms = 0

            def norm_stats(src, tiles):
                nonlocal norms
                for t in tiles:
                    step(dve.bn_stats(stats[:, t, :], src[:, t, :]))
                settle()
                for t in tiles:
                    step(dve.bn_aggr(mv[:, t, :], stats[:, t, :]))
                settle()
                lo, hi = tiles[0], tiles[-1] + 1
                dve.tensor_scalar(var_e[:, lo:hi], mv[:, lo:hi, 1], EPS, None, ALU.add).then_inc(var_ready, 1)
                norms += 1

            def norm_apply(dst, src, t):
                return dve.tensor_scalar(dst[:, t, :], src[:, t, :], mv[:, t, 0:1], rstd[:, t:t + 1],
                                         ALU.subtract, ALU.mult)

            def batch_tiles(b):
                return list(range(TB * b, TB * b + TB))

            def prep_lo(name, out_ap, hi_ap, n=512):
                dve.wait_ge(prep_act, prep.emptied(name, "A"))
                dve.tensor_tensor(out_ap, ps[:, prep.bank(name), 0:n], hi_ap, ALU.subtract).then_inc(prep_dve, 1)

            def first_norm(b):
                dve.wait_ge(x_loaded[b], 16)
                norm_stats(x_sb, batch_tiles(b))
                dve.wait_ge(rstd_ready, norms)
                for t in batch_tiles(b):
                    norm_apply(tok_sb, x_sb, t).then_inc(norm_ready, 1)

            first_norm(0)
            wT_fh = wT_hi[:, :, :].rearrange("p k n -> p (k n)").bitcast(F32)
            wT_fl = wT_lo[:, :, :].rearrange("p k n -> p (k n)")
            for i in range(3):
                prep_lo(f"W{i}", wT_fl[:, 512 * i:512 * i + 512], wT_fh[:, 512 * i:512 * i + 512])
            prep_lo("WO", woT_lo[:, :, :].rearrange("p k n -> p (k n)"),
                    woT_hi[:, :, :].rearrange("p k n -> p (k n)").bitcast(F32))
            dve.wait_ge(prep_act, prep.emptied("RW", "A"))
            dve.tensor_tensor(rwT[:, :, 1, :], ps[:, prep.bank("RW"), 0:KC * E].rearrange("p (k e) -> p k e", k=KC),
                              rwT[:, :, 0, :].bitcast(F32), ALU.subtract).then_inc(prep_dve, 1)
            dve.wait_ge(bias_loaded, 17)

            def prepare(name):
                kind, b, i = name[:-2], int(name[-2]), int(name[-1])
                bank = ps[:, prep.bank(name), :]
                if kind == "X":
                    prep_lo(name, tT_lo[:, i, S * b:S * b + S], tT_hi[:, i, S * b:S * b + S].bitcast(F32))
                if kind == "QK":
                    dve.wait_ge(prep_act, prep.emptied(name, "A"))
                    dve.scalar_tensor_tensor(out=qk_lo[:, i, :], in0=bank, scalar=bqk[:, i:i + 1],
                                             in1=qk_hi[:, i, :].bitcast(F32), op0=ALU.add, op1=ALU.subtract) \
                        .then_inc(prep_dve, 1)
                if kind == "V":
                    dve.wait_ge(prep_filled, prep.filled(name))
                    for n in range(2):
                        t = TB * b + 2 * i + n
                        ins = dve.tensor_tensor(v_sb[:, t, :, 0:HD],
                                                bank[:, D * n:D * n + D].rearrange("p (h d) -> p h d", d=HD),
                                                bv_bc[:, :].rearrange("p (h d) -> p h d", d=HD), ALU.add)
                    ins.then_inc(prep_dve, 1)
                if kind == "SQ" and prep.who[name] == "D":
                    dve.wait_ge(prep_filled, prep.filled(name))
                    dve.tensor_copy(q_op[b][:, i, :], bank).then_inc(prep_dve, 1)
                if kind == "SK" and "D" in prep.who[name]:
                    dve.wait_ge(prep_act, prep.emptied(name, "A"))
                    dve.tensor_scalar(k_op[b][1][:, i, :], bank, k_rows[:, 1:2], k_ones[:, 1:2],
                                      ALU.mult, ALU.add).then_inc(prep_dve, 1)

            for name, _ in first_units[5:]:
                if name == "SQ00":
                    dve.wait_ge(consts_ready, 3)
                prepare(name)
                if name == f"X0{KC - 1}":
                    first_norm(1)

            def maxima(g, banks):
                for i in banks:
                    heads, qt = m_plan()[i]
                    n = M_BANKS * g + i
                    w = P * (qt + 1)
                    dve.wait_ge(m_filled, n + 1)
                    if g >= 2:
                        dve.wait_ge(mT_filled, g - 1)
                    c = 4 * MT_ORDER[heads[0]] + qt
                    dve.tensor_reduce(rmax[:, g % 2, c:c + 4 * (len(heads) - 1) + 1:4],
                                      m_ps[n % 2][:, 0:w * len(heads)].rearrange("p (h c) -> p h c", c=w),
                                      AX.X, ALU.max).then_inc(m_reduced, 1)

            def max_lo(g):
                dve.wait_ge(mT_act, g + 1)
                dve.scalar_tensor_tensor(out=mT_lo[:, :], in0=t_ps[0:16, 0:P], scalar=-1.0,
                                         in1=mT_hi[:, :].bitcast(F32), op0=ALU.mult, op1=ALU.subtract) \
                    .then_inc(mT_dve, 1)

            def normalise(g):
                b, gi = divmod(g, NG)
                dve.wait_ge(o_filled, g + 1)
                blocks = t_ps.rearrange("p (q j c) -> p q j c", q=TB, j=4)
                settle()
                step(dve.reciprocal(orec[:, :].rearrange("p (q j) -> p q j", j=4), blocks[:, :, :, HD]))
                settle()
                dst = tok_sb[:, TB * b:TB * b + TB, 64 * gi:64 * gi + 64].rearrange("p q (j d) -> p q j d", d=HD)
                dve.tensor_tensor(dst, blocks[:, :, :, 0:HD],
                                  orec[:, :].rearrange("p (q j) -> p q j", j=4).unsqueeze(3).to_broadcast([P, TB, 4, HD]),
                                  ALU.mult).then_inc(o_normed, 1)

            def transposed_lo(b, name):
                for kc in range(KC):
                    unit = f"{name}{b}{kc}"
                    dve.wait_ge(post_act, post.emptied(unit, "A"))
                    dve.tensor_tensor(rowT_lo[b][:, kc, :], ps[:, post.bank(unit), :],
                                      rowT_hi[b][:, kc, :].bitcast(F32), ALU.subtract).then_inc(post_dve, 1)

            def projected(b):
                dve.wait_ge(bo_loaded, 16)
                for i in range(2):
                    name = f"OP{b}{i}"
                    t = TB * b + 2 * i
                    dve.wait_ge(post_filled, post.filled(name))
                    dve.tensor_tensor(tok_sb[:, t:t + 2, :], ps[:, post.bank(name), :].rearrange("p (t d) -> p t d", t=2),
                                      bo_bc[:, :].unsqueeze(1).to_broadcast([P, 2, D]), ALU.add).then_inc(post_dve, 1)
                dve.wait_ge(post_dve, post.emptied(f"OP{b}1", "D"))
                norm_stats(tok_sb, batch_tiles(b))

            def residual(b):
                dve.wait_ge(rstd_ready, norms)
                for t in batch_tiles(b):
                    step(norm_apply(tok_sb, tok_sb, t))
                settle()
                for t in batch_tiles(b):
                    step(dve.tensor_tensor(x_sb[:, t, :], x_sb[:, t, :], tok_sb[:, t, :], ALU.add))
                settle()
                norm_stats(x_sb, batch_tiles(b))

            def second_norm(b, tiles):
                dve.wait_ge(rstd_ready, norms)
                for t in tiles:
                    norm_apply(tok_sb, x_sb, t).then_inc(norm_ready, 1)

            def norm_shift(tiles):
                lo, hi = tiles[0], tiles[-1] + 1
                dve.wait_ge(rstd_ready, norms)
                dve.scalar_tensor_tensor(out=shift[:, lo:hi], in0=mv[:, lo:hi, 0], scalar=-1.0, in1=rstd[:, lo:hi],
                                         op0=ALU.mult, op1=ALU.mult).then_inc(shift_ready, 1)

            def residual_shared(b):
                for i, t in enumerate(batch_tiles(b)):
                    dve.wait_ge(act_normed, i + 1)
                    step(dve.tensor_tensor(x_sb[:, t, :], x_sb[:, t, :], tok_sb[:, t, :], ALU.add))
                settle()
                norm_stats(x_sb, batch_tiles(b))

            def take_logits(b):
                name = f"R{b}"
                dve.wait_ge(post_filled, post.filled(name))
                dve.tensor_reduce(logits[:, TB * b:TB * b + TB, :],
                                  ps[:, post.bank(name), 0:2 * TB * E].rearrange("p (t h e) -> p t e h", h=2, e=E),
                                  AX.X, ALU.add).then_inc(post_dve, 1)

            def shared_lo(n):
                for c in n:
                    dve.wait_ge(sh_hi, c + 1)
                    if c < 4:
                        k, half = divmod(c, 2)
                        o, r, h = (w[:, k, 512 * half:512 * half + 512] for w in (sgu_lo, sgu_raw, sgu_hi))
                    else:
                        o, r, h = (w[:, 2 * (c - 4):2 * (c - 4) + 2, :] for w in (sdn_lo, sdn_raw, sdn_hi))
                    dve.tensor_tensor(o, r, h.bitcast(F32), ALU.subtract).then_inc(sh_lo, 1)

            for s in range(LAG):
                for i in range(M_BANKS):
                    for name in mixed(s, i):
                        prepare(name)
                    maxima(s, (i,))
                    if s >= 1 and i == 2:
                        max_lo(s - 1)
            for s in range(LAG, GROUPS + LAG + 1):
                if s < GROUPS:
                    maxima(s, range(0, 3))
                if 0 <= s - 1 < GROUPS:
                    max_lo(s - 1)
                if s < GROUPS:
                    maxima(s, range(3, 9))
                if s == GROUPS:
                    transposed_lo(0, "A")
                if s == GROUPS + 1:
                    shared_lo([0, 1])
                    residual(0)
                if s == GROUPS + 2:
                    second_norm(0, batch_tiles(0))
                    shared_lo([2, 3])
                if 0 <= s - LAG - 1 < GROUPS:
                    normalise(s - LAG - 1)
                if s < GROUPS:
                    maxima(s, range(9, M_BANKS))
                if s == GROUPS:
                    projected(0)
                if s == GROUPS + 2:
                    transposed_lo(0, "X")
                    shared_lo([4, 5])

            def shared_hidden(b, ft):
                name = f"U{b}{ft}"
                dve.wait_ge(post_filled, post.filled(name))
                dve.wait_ge(post_act, post.emptied(f"G{b}{ft}", "A"))
                if ft >= 2 or b:
                    dve.wait_ge(hT_hi_ready, FC * b + ft - 1)
                    dve.wait_ge(hT_lo_ready, FC * b + ft - 1)
                dve.tensor_tensor(h_sb[:, ft % 2, :], ps[:, post.bank(name), :], silu_sb[:, ft % 2, :], ALU.mult) \
                    .then_inc(post_dve, 1)

            def shared_hidden_lo(b, ft):
                dve.wait_ge(hT_hi_ready, FC * b + ft + 1)
                dve.tensor_tensor(hT_lo[:, ft, :], h_sb[:, ft % 2, :], hT_hi[:, ft, :].bitcast(F32), ALU.subtract) \
                    .then_inc(hT_lo_ready, 1)

            def routing():
                e_bc = [P, NT, E]
                dve.wait_ge(post_dve, post.emptied("R1", "D"))
                dve.wait_ge(rconsts_ready, 1)
                dve.tensor_reduce(top[:, :], logits[:, :, :], AX.X, ALU.max).then_inc(top_ready, 1)
                dve.wait_ge(top_ready, 1)
                step(dve.tensor_tensor(hit[:, :, :], logits[:, :, :], top[:, :].unsqueeze(2).to_broadcast(e_bc), ALU.is_equal))
                settle()
                step(dve.tensor_tensor(hit[:, :, :], hit[:, :, :], desc[:, :].unsqueeze(1).to_broadcast(e_bc), ALU.mult))
                settle()
                step(dve.tensor_reduce(first[:, :], hit[:, :, :], AX.X, ALU.max))
                settle()
                step(dve.tensor_tensor(onehot[:, :, :], hit[:, :, :], first[:, :].unsqueeze(2).to_broadcast(e_bc), ALU.is_equal))
                settle()
                dve.tensor_copy(onehot_b[:, :, :], onehot[:, :, :]).then_inc(onehot_ready, 1)

            def slots():
                dve.wait_ge(post_filled, post.filled("RK"))
                bank = ps[:, post.bank("RK"), :]
                ranks = bank[:, 0:NT * E].rearrange("p (t e) -> p t e", e=E)
                counts = bank[:, NT * E:NT * E + E]
                step(dve.tensor_tensor(over[:, :, :], counts.unsqueeze(2).to_broadcast([P, E, E]),
                                       thr[:, :].unsqueeze(1).to_broadcast([P, E, E]), ALU.is_gt))
                settle()
                step(dve.tensor_reduce(n_tiles[:, :], over[:, :, :], AX.X, ALU.add))
                settle()
                step(dve.tensor_tensor_scan(ends[:, :], ones_e[:, :], n_tiles[:, :], 0.0, ALU.mult, ALU.add))
                settle()
                step(dve.tensor_tensor(base_t[:, :], ends[:, :], n_tiles[:, :], ALU.subtract))
                settle()
                dve.scalar_tensor_tensor(out=where[:, :, :], in0=base_t[:, :].unsqueeze(1).to_broadcast([P, NT, E]),
                                         scalar=float(P), in1=ranks, op0=ALU.mult, op1=ALU.add).then_inc(post_dve, 1)
                dve.wait_ge(post_dve, post.emptied("RK", "D"))
                step(dve.tensor_tensor(where[:, :, :], where[:, :, :], onehot[:, :, :], ALU.mult))
                settle()
                step(dve.tensor_reduce(pos_f[:, :], where[:, :, :], AX.X, ALU.add))
                settle()
                dve.tensor_copy(pos_u[:, :], pos_f[:, :]).then_inc(pos_ready, 1)
                step(dve.tensor_tensor(past[:, :, :], ends[:, :].unsqueeze(1).to_broadcast([P, 16, E]),
                                       slot_no[:, :].unsqueeze(2).to_broadcast([P, 16, E]), ALU.is_le))
                settle()
                step(dve.tensor_reduce(own_f[:, :], past[:, :, :], AX.X, ALU.add))
                settle()
                dve.tensor_scalar(own_u[:, :], own_f[:, :], float(E - 1), None, ALU.min).then_inc(owner_ready, 1)

            def gated():
                dve.wait_ge(gate_ready, 1)
                for t in range(NT):
                    dve.tensor_scalar(tok_sb[:, t, :], tok_sb[:, t, :], gate[:, t:t + 1], None, ALU.mult) \
                        .then_inc(gated_ready, 1)

            def shared_units(b, fts):
                for ft in fts:
                    shared_hidden(b, ft)
                    if ft >= 1:
                        shared_hidden_lo(b, ft - 1)
                    if ft == FC - 1:
                        shared_hidden_lo(b, ft)

            take_logits(0)
            transposed_lo(1, "A")
            shared_units(0, [0])
            projected(1)
            shared_units(0, [1])
            norm_shift(batch_tiles(1))
            shared_units(0, [2])
            residual_shared(1)
            shared_units(0, [3])
            norm_shift(batch_tiles(1)[2:])
            second_norm(1, batch_tiles(1)[:2])
            transposed_lo(1, "X")
            take_logits(1)
            routing()
            gated()
            slots()
            shared_units(1, [0])
            shared_units(1, [1, 2, 3])

            def slot_mul(s):
                name = f"u{s}"
                dve.wait_ge(post_filled, post.filled(name))
                dve.wait_ge(post_act, post.emptied(f"g{s}", "A"))
                if s >= 2:
                    dve.wait_ge(post_filled, post.filled(f"ht{s - 2}"))
                else:
                    dve.wait_ge(hT_lo_ready, NB * FC)
                dve.tensor_tensor(h_sb[:, s % 2, :], ps[:, post.bank(name), :], silu_sb[:, s % 2, :], ALU.mult) \
                    .then_inc(post_dve, 1)

            def take_output(s):
                i, y = s % NT, ysl[:, s % 4, :]
                if s == 0:
                    dve.wait_ge(scattered, 16 * NT)
                if s >= 4:
                    dve.wait_ge(out_scattered[s % 4], 16 * (s // 4))
                dve.wait_ge(ysh_loaded[s % 2], 16 * (s // 2 + 1))
                dve.wait_ge(post_filled, post.filled(f"dn{s}"))
                dve.tensor_tensor(y, ps[:, post.bank(f"dn{s}"), 0:D], ysh_in[:, s % 2, :], ALU.add).then_inc(post_dve, 1)
                dve.wait_ge(post_dve, post.emptied(f"dn{s}", "D"))
                step(dve.bn_stats(stats[:, i, :], y))
                settle()
                step(dve.bn_aggr(mv[:, i, :], stats[:, i, :]))
                settle()
                dve.tensor_scalar(var_e[:, i:i + 1], mv[:, i, 1:2], EPS, None, ALU.add).then_inc(var_ready, 1)

            def last_norm(s):
                i, y = s % NT, ysl[:, s % 4, :]
                dve.wait_ge(rstd_ready, norms + s + 1)
                dve.tensor_scalar(y, y, mv[:, i, 0:1], rstd[:, i:i + 1], ALU.subtract, ALU.mult).then_inc(last_norm_ready, 1)

            def slot_xT_lo(s):
                if s >= 2:
                    dve.wait_ge(post_filled, post.filled(f"u{s - 2}"))
                name = f"xt{s}"
                dve.wait_ge(post_act, post.emptied(name, "A"))
                dve.tensor_tensor(xinT_lo[:, s % 2, :, :].rearrange("p k t -> p (k t)"), ps[:, post.bank(name), 0:KC * P],
                                  xinT_hi[:, s % 2, :, :].rearrange("p k t -> p (k t)").bitcast(F32), ALU.subtract) \
                    .then_inc(post_dve, 1)

            def slot_weights_lo(s, e, half):
                cols = slice(F * half, F * half + F)
                dve.wait_ge(wsl_hi_ready, 2 * s + half + 1)
                dve.tensor_tensor(wsl_lo[s % 2][:, :, cols], owned_half(e, half),
                                  wsl_hi[s % 2][:, :, cols].bitcast(F32), ALU.subtract).then_inc(wsl_lo_ready, 1)

            dve.wait_ge(wgu_loaded, 16 * E)
            dve.wait_ge(owner_ready, 1)
            owners = slot_owners(ENGINE.DVE)
            for s in range(2):
                e = owners[s]
                slot_weights_lo(s, e, 0)
                slot_weights_lo(s, e, 1)
                if s == 0:
                    slot_xT_lo(0)
            slot_mul(0)
            slot_xT_lo(1)
            for s in range(SLOTS):
                if s >= 1:
                    take_output(s - 1)
                if s + 2 < SLOTS:
                    e = owners[s + 2]
                    slot_weights_lo(s + 2, e, 0)
                    slot_xT_lo(s + 2)
                if s >= 1:
                    last_norm(s - 1)
                if s + 1 < SLOTS:
                    slot_mul(s + 1)
                if s + 2 < SLOTS:
                    slot_weights_lo(s + 2, e, 1)
            take_output(SLOTS - 1)
            last_norm(SLOTS - 1)

        @block.tensor
        def _(pe):
            def mm(o, lhsT, rhs, start, stop):
                return pe.matmul(o, lhsT, rhs, start=start, stop=stop)

            def split_mm(o, pairs, start=True, stop=True):
                n, total = 0, 3 * len(pairs)
                for (a_hi, a_lo), (b_hi, b_lo) in pairs:
                    for a, c in ((a_hi, b_hi), (a_hi, b_lo), (a_lo, b_hi)):
                        last = mm(o, a, c, start and n == 0, stop and n == total - 1)
                        n += 1
                return last

            def enter_prep(name):
                prev = prep.before(name)
                if prev:
                    for engine, s in (("A", prep_act), ("D", prep_dve)):
                        if engine in prep.who[prev]:
                            pe.wait_ge(s, prep.emptied(prev, engine))
                return ps[:, prep.bank(name), :]

            pe.wait_ge(consts_ready, 1)
            pe.wait_ge(w_loaded, 64)
            for w in range(3):
                bank = enter_prep(f"W{w}")
                for i in range(4):
                    kc, r = divmod(4 * w + i, 6)
                    last = pe.transpose(bank[:, P * i:P * i + P], wqkv_raw[:, r, kc * P:kc * P + P], ident[:, :])
                last.then_inc(prep_filled, 1)
            bank = enter_prep("WO")
            for i in range(4):
                kc, r = divmod(i, 2)
                last = pe.transpose(bank[:, P * i:P * i + P], wout_raw[:, r, kc * P:kc * P + P], ident[:, :])
            last.then_inc(prep_filled, 1)
            bank = enter_prep("RW")
            for kc in range(KC):
                last = pe.transpose(bank[:, E * kc:E * kc + E], rw_sb[0:E, kc * P:kc * P + P], ident[0:E, 0:E])
            last = pe.transpose(bank[:, KC * E:KC * E + 4], bqk_raw[0:4, :], ident[0:4, 0:4])
            last.then_inc(prep_filled, 1)

            def hl(hi, lo, *index):
                return hi[index], lo[index]

            every = slice(None)

            def prepare(name):
                kind, b, i = name[:-2], int(name[-2]), int(name[-1])
                if kind == "X":
                    pe.wait_ge(norm_ready, TB * (b + 1))
                    bank = enter_prep(name)
                    for t in range(TB):
                        last = pe.transpose(bank[:, P * t:P * t + P], tok_sb[:, TB * b + t, i * P:i * P + P], ident[:, :])
                if kind == "QK":
                    bank = enter_prep(name)
                    pe.wait_ge(prep_dve, prep.emptied(f"X{b}1", "D"))
                    last = split_mm(bank, [(hl(wT_hi, wT_lo, every, kc, slice(i * P, i * P + P)),
                                            hl(tT_hi, tT_lo, every, kc, slice(S * b, S * b + S))) for kc in range(KC)])
                if kind == "V":
                    bank = enter_prep(name)
                    pe.wait_ge(prep_dve, prep.emptied(f"X{b}1", "D"))
                    for n in range(2):
                        t = TB * b + 2 * i + n
                        last = split_mm(bank[:, D * n:D * n + D],
                                        [(hl(tT_hi, tT_lo, every, kc, slice(t * P, t * P + P)),
                                          hl(wT_hi, wT_lo, every, kc, slice(2 * D, 3 * D))) for kc in range(KC)])
                if kind in ("SQ", "SK"):
                    m = 0 if kind == "SQ" else 2
                    mt = m + i // 4
                    bank = enter_prep(name)
                    pe.wait_ge(consts_ready, 3)
                    pe.wait_ge(prep_dve, prep.emptied(f"QK{b}{mt}", "D"))
                    mm(bank, sel[:, m, i % 4, :], qk_hi[:, mt, :], True, False)
                    last = mm(bank, sel[:, m + 1, i % 4, :], qk_lo[:, mt, :], False, True)
                last.then_inc(prep_filled, 1)

            for name, _ in first_units[5:]:
                prepare(name)

            def prepared(name):
                pe.wait_ge(prep_act, prep.emptied(name, "A"))
                pe.wait_ge(prep_dve, prep.emptied(name, "D"))

            def m_scores(g, banks):
                b, gi = divmod(g, NG)
                if banks[0] == 0:
                    prepared(f"SK{b}{2 * gi + 1}")
                for i in banks:
                    heads, qt = m_plan()[i]
                    n = M_BANKS * g + i
                    if n >= 2:
                        pe.wait_ge(m_reduced, n - 1)
                    w = P * (qt + 1)
                    for k, j in enumerate(heads):
                        pair = 2 * gi + j // 2
                        mm(m_ps[n % 2][:, w * k:w * k + w], q_op[b][:, pair, qt * P:qt * P + P],
                           k_op[b][j % 2][:, pair, 0:w], k == 0, False)
                    diagonal = m_ps[n % 2][:, 0:w * len(heads)].rearrange("p (h c) -> p h c", c=w)[:, :, w - P:w]
                    masks = mask[:, :].unsqueeze(1).to_broadcast([P, len(heads), P])
                    mm(diagonal, ident_b[:, :], masks, False, True).then_inc(m_filled, 1)

            def max_transpose(g):
                pe.wait_ge(m_reduced, M_BANKS * (g + 1))
                if g >= LAG + 1:
                    pe.wait_ge(o_normed, g - LAG)
                pe.transpose(t_ps[0:16, 0:P], rmax[:, g % 2, :], ident[:, :]).then_inc(mT_filled, 1)

            def st_scores(g, u):
                b, gi = divmod(g, NG)
                n = 5 * g + u
                if u == 0:
                    pe.wait_ge(max_placed, 64 * (g + 1))
                if n == 0:
                    prepared(LAST_PREP)
                if n >= 2:
                    pe.wait_ge(exp_done, n - 1)
                opened = set()
                plan = st_plan(u)
                for k, (j, kt, i, c) in enumerate(plan):
                    pair = 2 * gi + j // 2
                    w = S - kt * P
                    closes = all(i2 != i for _, _, i2, _ in plan[k + 1:])
                    last = mm(st_ps[n % 2][:, i, c:c + w], k_op[b][j % 2][:, pair, kt * P:kt * P + P],
                              q_op[b][:, pair, kt * P:S], i not in opened, closes)
                    opened.add(i)
                last.then_inc(st_filled, 1)

            def pv(g, kt, units):
                b, gi = divmod(g, NG)
                pe.wait_ge(causal_done, 5 * g + units)
                if kt == 0 and g >= 1:
                    pe.wait_ge(oT_copied, g)
                for j in range(4):
                    u, c = pt_place(j, kt)
                    w = S - kt * P
                    last = pe.matmul(o_ps[32 * j:32 * j + 32, kt * P:S], v_sb[:, TB * b + kt, 4 * gi + j, :],
                                     pT[:, u, c:c + w], start=kt == 0, stop=kt == 2, tile_position=(0, 32 * j))
                last.then_inc(pv_done, 1)

            def o_transposes(g):
                pe.wait_ge(oT_copied, g + 1)
                pe.wait_ge(mT_dve, min(g + LAG + 1, GROUPS))
                if g >= 1:
                    pe.wait_ge(o_normed, g)
                for qt in range(TB):
                    last = pe.transpose(t_ps[:, P * qt:P * qt + P], oT_sb[:, g % 2, P * qt:P * qt + P], ident[:, :])
                last.then_inc(o_filled, 1)

            def enter_post(name):
                prev = post.before(name)
                if prev:
                    for engine, s in (("A", post_act), ("D", post_dve)):
                        if engine in post.who[prev]:
                            pe.wait_ge(s, post.emptied(prev, engine))
                return ps[:, post.bank(name), :]

            def transposed(b, name):
                for kc in range(KC):
                    bank = enter_post(f"{name}{b}{kc}")
                    for i in range(TB):
                        last = pe.transpose(bank[:, P * i:P * i + P], tok_sb[:, TB * b + i, kc * P:kc * P + P], ident[:, :])
                    last.then_inc(post_filled, 1)

            def out_projection(b):
                for i in range(2):
                    bank = enter_post(f"OP{b}{i}")
                    pe.wait_ge(post_dve, post.emptied(f"A{b}1", "D"))
                    for n in range(2):
                        c = P * (2 * i + n)
                        last = split_mm(bank[:, D * n:D * n + D],
                                        [(hl(rowT_hi[b], rowT_lo[b], every, kc, slice(c, c + P)),
                                          hl(woT_hi, woT_lo, every, kc, every)) for kc in range(KC)])
                    last.then_inc(post_filled, 1)

            def router(b):
                bank = enter_post(f"R{b}")
                pe.wait_ge(post_dve, post.emptied(f"X{b}1", "D"))
                for i in range(TB):
                    for kc in range(KC):
                        toks = slice(i * P, i * P + P)
                        mm(bank[:, 2 * E * i:2 * E * i + 2 * E], rowT_hi[b][:, kc, toks],
                           rwT[:, kc, :, :].rearrange("p h e -> p (h e)"), kc == 0, False)
                        last = mm(bank[:, 2 * E * i:2 * E * i + E], rowT_lo[b][:, kc, toks], rwT[:, kc, 0, :],
                                  False, kc == KC - 1)
                last.then_inc(post_filled, 1)

            for s in range(LAG):
                for i in range(M_BANKS):
                    for name in mixed(s, i):
                        prepare(name)
                    m_scores(s, (i,))
                    if s >= 1 and i == 1:
                        max_transpose(s - 1)
            for s in range(LAG, GROUPS + LAG + 1):
                e, m = s - LAG, s
                on_e, on_m = 0 <= e < GROUPS, m < GROUPS
                if on_e:
                    st_scores(e, 0)
                if on_m:
                    m_scores(m, (0, 1))
                if 0 <= e - 1 < GROUPS:
                    pv(e - 1, 1, 4)
                    pv(e - 1, 3, 4)
                if 0 <= s - 1 < GROUPS:
                    max_transpose(s - 1)
                if on_m:
                    m_scores(m, (2,))
                if on_e:
                    st_scores(e, 1)
                if 0 <= e - 1 < GROUPS:
                    pv(e - 1, 2, 5)
                if s == GROUPS:
                    pe.wait_ge(m_reduced, M_BANKS * GROUPS)
                    transposed(0, "A")
                if on_m:
                    m_scores(m, (3, 4))
                if on_e:
                    st_scores(e, 2)
                    pv(e, 0, 2)
                if on_m:
                    m_scores(m, (5, 6))
                if on_e:
                    st_scores(e, 3)
                if on_m:
                    m_scores(m, (7,))
                if 0 <= e - 1 < GROUPS:
                    o_transposes(e - 1)
                if on_m:
                    m_scores(m, (8,))
                if on_e:
                    st_scores(e, 4)
                if s == GROUPS:
                    out_projection(0)
                if s == GROUPS + 2:
                    pe.wait_ge(norm_ready, TB * NB + TB)
                    transposed(0, "X")
                if on_m:
                    m_scores(m, (9, 10))

            def ranks():
                bank = enter_post("RK")
                pe.wait_ge(onehot_ready, 1)
                oh = onehot_b[:, :, :].rearrange("p t e -> p (t e)")
                mm(bank[:, 0:NT * E], lt_b[:, :], oh, True, False)
                for k in range(1, NT):
                    mm(bank[:, E * k:NT * E], ones_b[:, :], oh[:, 0:(NT - k) * E], False, False)
                for k in range(NT):
                    last = mm(bank[:, NT * E:NT * E + E], ones_b[:, :], oh[:, E * k:E * k + E], False, k == NT - 1)
                last.then_inc(post_filled, 1)

            def hidden_half(b, ft, n):
                c = F * n + ft * P
                split_mm(enter_post(f"{'GU'[n]}{b}{ft}"),
                         [(hl(sgu_hi, sgu_lo, every, kc, slice(c, c + P)), hl(rowT_hi[b], rowT_lo[b], every, kc, every))
                          for kc in range(KC)]).then_inc(post_filled, 1)

            def hidden(b, fts):
                for ft in fts:
                    hidden_half(b, ft, 0)
                    hidden_half(b, ft, 1)

            def down(b, i):
                bank = enter_post(f"DN{b}{i}")
                for ft in range(FC):
                    pe.wait_ge(hT_lo_ready, FC * b + ft + 1)
                    for n in range(2):
                        c = P * (2 * i + n)
                        last = split_mm(bank[:, D * n:D * n + D], [(hl(hT_hi, hT_lo, every, ft, slice(c, c + P)),
                                                                    hl(sdn_hi, sdn_lo, every, ft, every))],
                                        ft == 0 and n == 0, ft == FC - 1 and n == 1)
                last.then_inc(post_filled, 1)

            pe.wait_ge(exp_done, 5 * GROUPS)
            router(0)
            pe.wait_ge(sh_lo, 6)
            pe.wait_ge(o_normed, GROUPS)
            transposed(1, "A")
            hidden(0, [0])
            out_projection(1)
            hidden(0, [1, 2, 3])
            down(0, 0)
            pe.wait_ge(norm_ready, 2 * TB * NB - 2)
            pe.wait_ge(act_normed, TB + 2)
            transposed(1, "X")
            down(0, 1)
            router(1)
            hidden_half(1, 0, 0)
            ranks()
            hidden_half(1, 0, 1)
            hidden(1, [1, 2, 3])
            down(1, 0)
            down(1, 1)

            pe.wait_ge(owner_ready, 1)
            pe.wait_ge(wgu_loaded, 16 * E)
            pe.wait_ge(wdn_loaded, 16 * E)

            def slot_xT(s):
                bank = enter_post(f"xt{s}")
                pe.wait_ge(xin_loaded[s % 5], 16 * (s // 5 + 1))
                for kc in range(KC):
                    last = pe.transpose(bank[:, P * kc:P * kc + P], xin[:, s % 5, D + kc * P:D + kc * P + P], ident[:, :])
                last.then_inc(post_filled, 1)

            def slot_half(s, half):
                name = f"{'gu'[half]}{s}"
                bank = enter_post(name)
                pe.wait_ge(post_dve, post.emptied(f"xt{s}", "D"))
                pe.wait_ge(wsl_lo_ready, 2 * s + half + 1)
                split_mm(bank, [(hl(xinT_hi, xinT_lo, every, s % 2, kc, every),
                                 hl(wsl_hi[s % 2], wsl_lo[s % 2], every, kc, slice(F * half, F * half + F)))
                                for kc in range(KC)]).then_inc(post_filled, 1)

            def slot_hT(s):
                bank = enter_post(f"ht{s}")
                pe.wait_ge(post_dve, post.emptied(f"u{s}", "D"))
                for k in range(FC):
                    last = pe.transpose(bank[:, P * k:P * k + P], h_sb[:, s % 2, P * k:P * k + P], ident[:, :])
                last.then_inc(post_filled, 1)

            def slot_down(s, e):
                bank = enter_post(f"dn{s}")
                pe.wait_ge(post_act, post.emptied(f"ht{s}", "A"))
                for k in range(FC):
                    last = mm(bank[:, 0:D], rhT[:, s % 2, k, :],
                              wdn_sb[:, bass.ds(e * (FC * D) + k * D, D)], k == 0, k == FC - 1)
                last.then_inc(post_filled, 1)

            owners = slot_owners(ENGINE.PE)
            slot_xT(0)
            slot_half(0, 0)
            slot_half(0, 1)
            slot_xT(1)
            for s in range(SLOTS):
                if s + 1 < SLOTS:
                    slot_half(s + 1, 0)
                slot_hT(s)
                if s + 2 < SLOTS:
                    slot_xT(s + 2)
                if s + 1 < SLOTS:
                    slot_half(s + 1, 1)
                slot_down(s, owners[s])


INPUTS = ["L0_attn_x", "L0_attn_Wqkv", "L0_attn_bqkv", "L0_attn_Wout", "L0_attn_bout", "L0_ffn_router_w",
          "L0_ffn_w_gate_up", "L0_ffn_w_down", "L0_ffn_shared_gate_up", "L0_ffn_shared_down"]


def kernel(**inputs):
    import numpy as np
    import concourse.bacc as bacc
    from concourse.bass_utils import run_bass_kernel_spmd

    nc = bacc.Bacc("TRN2", target_bir_lowering=False, num_devices=1)
    arrays, args = {}, []
    for name in INPUTS:
        a = np.ascontiguousarray(inputs[name])
        arrays[name] = a
        args.append(nc.dram_tensor(name, a.shape, mybir.dt.from_np(a.dtype), kind="ExternalInput").ap())
    out = nc.dram_tensor("out", inputs["L0_attn_x"].shape, F32, kind="ExternalOutput").ap()
    build_block(nc, *args, out)
    r = run_bass_kernel_spmd(nc, [arrays], core_ids=[0])
    return r.results[0]["out"]
```
